# Optimizing a Trainium2 kernel written in Bass

```python
import numpy as np
import jax
import jax.numpy as jnp

def _softmax(x, axis=-1):
    return jax.nn.softmax(x, axis=axis)

def _gelu(x):
    return jax.nn.gelu(x, approximate=True)

def _silu(x):
    return jax.nn.silu(x)

def _sigmoid(x):
    return jax.nn.sigmoid(x)

def _layernorm(x, axis=-1, eps=1e-05):
    m = jnp.mean(x, axis=axis, keepdims=True)
    v = jnp.var(x, axis=axis, keepdims=True)
    return (x - m) / jnp.sqrt(v + eps)

def _scatter_add(tgt, idx, src, axis=0):
    return tgt.at[idx].add(src)

def _segment_sum(src, seg, n):
    return jax.ops.segment_sum(src, seg, n)
kernel_name = 'mk_rec_standalone_d1_rec_r8_f56a24'

def setup_inputs(seed: int=0):
    np.random.seed(seed)
    _w = jnp.asarray

    def _rec_inputs():
        import jax
        import jax.numpy as jnp
        _rk = jax.random.key(seed)
        r_users = jax.random.randint(jax.random.fold_in(_rk, 1), (1024,), 19, 49991, jnp.int32)
        return r_users
    r_users = _rec_inputs()

    def _L0_rec_setup():
        import jax, jax.numpy as jnp
        import numpy as np
        NUM_USERS = 6250
        NUM_ITEMS = 12500
        N_NODES = NUM_USERS + NUM_ITEMS
        NNZ = 250000
        LATENT = 64
        MINI = 16
        N_LAYERS = 3
        BATCH = 1024

        def _propagate(all_emb, rows, cols, vals):
            acc = all_emb
            x = all_emb
            for _ in range(N_LAYERS):
                x = jax.ops.segment_sum(vals[:, None] * x[cols], rows, num_segments=N_NODES)
                acc = acc + x
            return acc / (N_LAYERS + 1)

        def _upsample_nearest(x):
            idx = jnp.arange(LATENT) * MINI // LATENT
            return x[:, idx]
        key = jax.random.key(seed)
        ks = jax.random.split(key, 10)
        return {'emb_user': 0.1 * jax.random.normal(ks[0], (NUM_USERS, LATENT), jnp.float32), 'emb_item': 0.1 * jax.random.normal(ks[1], (NUM_ITEMS, LATENT), jnp.float32), 'bias_user': jnp.zeros((NUM_USERS, 1), jnp.float32), 'bias_item': jnp.zeros((NUM_ITEMS, 1), jnp.float32), 'mm_emb_user': 0.1 * jax.random.normal(ks[2], (NUM_USERS, MINI), jnp.float32), 'mm_emb_item': 0.1 * jax.random.normal(ks[3], (NUM_ITEMS, MINI), jnp.float32), 'graph_vals': jax.random.uniform(ks[4], (NNZ,), jnp.float32) / 32.0, 'users': jax.random.randint(ks[5], (BATCH,), 0, NUM_USERS, jnp.int32), 'graph_rows': jax.random.randint(ks[6], (NNZ,), 0, N_NODES, jnp.int32), 'graph_cols': jax.random.randint(ks[7], (NNZ,), 0, N_NODES, jnp.int32)}
    _L0_rec_all = _L0_rec_setup()
    _L0_rec_in = {k: v for k, v in _L0_rec_all.items() if k in ('emb_user', 'emb_item', 'bias_user', 'bias_item', 'mm_emb_user', 'mm_emb_item', 'graph_vals', 'graph_rows', 'graph_cols')}
    del _L0_rec_all
    return {'r_users': r_users, 'L0_rec_emb_user': _L0_rec_in['emb_user'], 'L0_rec_emb_item': _L0_rec_in['emb_item'], 'L0_rec_bias_user': _L0_rec_in['bias_user'], 'L0_rec_bias_item': _L0_rec_in['bias_item'], 'L0_rec_mm_emb_user': _L0_rec_in['mm_emb_user'], 'L0_rec_mm_emb_item': _L0_rec_in['mm_emb_item'], 'L0_rec_graph_vals': _L0_rec_in['graph_vals'], 'L0_rec_graph_rows': _L0_rec_in['graph_rows'], 'L0_rec_graph_cols': _L0_rec_in['graph_cols']}

def reference(r_users, L0_rec_emb_user, L0_rec_emb_item, L0_rec_bias_user, L0_rec_bias_item, L0_rec_mm_emb_user, L0_rec_mm_emb_item, L0_rec_graph_vals, L0_rec_graph_rows, L0_rec_graph_cols):
    import jax
    import jax.numpy as jnp

    def _L0_rec_ref(emb_user, emb_item, bias_user, bias_item, mm_emb_user, mm_emb_item, graph_vals, users, graph_rows, graph_cols):
        import jax, jax.numpy as jnp
        import numpy as np
        NUM_USERS = 6250
        NUM_ITEMS = 12500
        N_NODES = NUM_USERS + NUM_ITEMS
        NNZ = 250000
        LATENT = 64
        MINI = 16
        N_LAYERS = 3
        BATCH = 1024

        def _propagate(all_emb, rows, cols, vals):
            acc = all_emb
            x = all_emb
            for _ in range(N_LAYERS):
                x = jax.ops.segment_sum(vals[:, None] * x[cols], rows, num_segments=N_NODES)
                acc = acc + x
            return acc / (N_LAYERS + 1)

        def _upsample_nearest(x):
            idx = jnp.arange(LATENT) * MINI // LATENT
            return x[:, idx]
        all_emb = jnp.concatenate([emb_user, emb_item], axis=0)
        light_out = _propagate(all_emb, graph_rows, graph_cols, graph_vals)
        all_users, all_items = (light_out[:NUM_USERS], light_out[NUM_USERS:])
        mm_all = jnp.concatenate([mm_emb_user, mm_emb_item], axis=0)
        mm_out = _propagate(mm_all, graph_rows, graph_cols, graph_vals)
        mm_users, mm_items = (mm_out[:NUM_USERS], mm_out[NUM_USERS:])
        users_emb = all_users[users] + _upsample_nearest(mm_users[users])
        items_emb = all_items + _upsample_nearest(mm_items)
        rating = users_emb @ items_emb.T
        rating = rating + bias_user[users] + bias_item.T
        return jax.nn.sigmoid(rating)
    y = _L0_rec_ref(L0_rec_emb_user, L0_rec_emb_item, L0_rec_bias_user, L0_rec_bias_item, L0_rec_mm_emb_user, L0_rec_mm_emb_item, L0_rec_graph_vals, r_users, L0_rec_graph_rows, L0_rec_graph_cols)
    return y

_drawn_inputs = setup_inputs


def setup_inputs(seed=0):
    import zlib

    import numpy as np

    out = dict(_drawn_inputs(seed))
    spreads = {'L0_rec_bias_user': (0.0, 0.44), 'L0_rec_bias_item': (0.0, 0.1)}
    factors = {'L0_rec_emb_user': 8.0,
     'L0_rec_emb_item': 8.0,
     'L0_rec_mm_emb_user': 8.0,
     'L0_rec_mm_emb_item': 8.0,
     'L0_rec_graph_vals': 8.0}
    for name, (base, spread) in spreads.items():
        noise = np.random.default_rng([zlib.crc32(name.encode()), seed]).standard_normal(out[name].shape)
        drawn = base * np.exp(spread * noise) if base else spread * noise
        out[name] = jnp.asarray(drawn.astype(out[name].dtype))
    for name, factor in factors.items():
        out[name] = (out[name] * factor).astype(out[name].dtype)
    return out
```

```python
from contextlib import ExitStack

import concourse.bass as bass
from concourse import mybir

FP32 = mybir.dt.float32
BF16 = mybir.dt.bfloat16
I32 = mybir.dt.int32
ALU = mybir.AluOpType
ACT = mybir.ActivationFunctionType
AX = mybir.AxisListType

P = 128
USERS, ITEMS, F, MINI = 6250, 12500, 64, 16
NODES = USERS + ITEMS
NNZ = 250000
BATCH = 1024
LAYERS = 3
TILES = -(-NODES // P)
TABLE = TILES * P
ZERO_ROW = TABLE - 1

SG = 7
SORT_ITERS = -(-NNZ // (P * 2 * SG))
T = SORT_ITERS * 2 * SG
EDGES = T * P
LAST_E = NNZ - (P - 1) * T

UNITS = 2
UNIT = P // UNITS
LG = 8
RING = 2 * LG
K_LEAST = -(-(EDGES + TILES * (UNIT - 1)) // P)
LAYER_ITERS = -(-K_LEAST // RING)
K = LAYER_ITERS * RING
UCOLS = -(-K * UNITS // P)
R_SLOTS = 8
PS_SLOTS = 4
UTILES = -(-USERS // P)
U_LANES = USERS - (UTILES - 1) * P
I_FIRST = UTILES * P - USERS
I_TILES = (NODES // P) - UTILES
I_LAST = NODES - (NODES // P) * P
NB = 500
MT = BATCH // P


def build(nc, users, emb_u, emb_i, bias_u, bias_i, mm_u, mm_i, vals, rows, cols, out):
    table = nc.dram_tensor("table", [TABLE, F], FP32)
    slots = nc.dram_tensor("slots", [P * K, 4], I32)
    unit_map = nc.dram_tensor("unit_map", [P, UCOLS], I32)
    user_rows = nc.dram_tensor("user_rows", [P * UTILES, F], FP32)
    table_v = table.rearrange("(p t) f -> p (t f)", p=P)
    slots_v = slots.rearrange("(p k) w -> p (k w)", p=P)
    out_v = out.rearrange("(p m) n -> p m n", m=MT)

    with ExitStack() as ctx:
        def sb(name, shape, dt):
            return ctx.enter_context(nc.sbuf_tensor(name, shape, dt))

        def sem(name):
            return ctx.enter_context(nc.semaphore(name))

        arena = sb("arena", [P, ITEMS], FP32)
        payload = arena[:, 0:4 * T].rearrange("p (t w) -> p t w", w=4)
        payload_i = payload.bitcast(I32)
        rows_i = arena[:, 4 * T:5 * T].bitcast(I32)
        cols_i = arena[:, 5 * T:6 * T].bitcast(I32)
        below = arena[:, 4 * T:6 * T].bitcast(BF16)[:, 0:UCOLS * TILES].rearrange(
            "p (j t) -> p j t", t=TILES)
        items_t = arena[0:F + 1, :]
        rated = sb("rated", [P, MT, NB], FP32)
        flat = rated[:, :, :].rearrange("p m n -> p (m n)")
        vals_f = flat[:, 0:T]
        bits = flat[:, T:2 * T].bitcast(I32)
        new = sb("new", [P, TILES * F], FP32)
        total = sb("total", [P, TILES * F], FP32)
        new3 = new[:, :].rearrange("p (t f) -> p t f", f=F)
        mini = sb("mini", [P, TILES, MINI], FP32)
        fill_sb = sb("fill_sb", [P, K // RING, 4], I32)
        unit_off = sb("unit_off", [1, P * UCOLS], I32)
        gathered = sb("gathered", [P, RING, F], FP32)
        spread = sb("spread", [P, R_SLOTS, P], FP32)
        ring = sb("ring", [P, 2, LG, 4], I32)
        ring_f = ring[:, :, :, :].bitcast(FP32)
        pay = sb("pay", [P, 2, SG, 4], I32)
        pay_f = pay[:, :, :, :].bitcast(FP32)
        keys = sb("keys", [P, 2, SG], FP32)
        onehot = sb("onehot", [P, 2 * SG, TILES], BF16)
        picked = sb("picked", [P, TILES], BF16)
        rank = sb("rank", [P, 2, SG], FP32)
        rank_i = sb("rank_i", [P, SG], I32)
        rank_lo = sb("rank_lo", [P, SG], I32)
        rank_hi = sb("rank_hi", [P, SG], I32)
        place = sb("place", [P, 2, SG], I32)
        iota_i = sb("iota_i", [P, TILES], I32)
        lane_i = sb("lane_i", [P, 1], I32)
        lane_f = sb("lane_f", [P, 1], FP32)
        iota_t = sb("iota_t", [P, TILES], BF16)
        iota_l = sb("iota_l", [P, P], FP32)
        ident = sb("ident", [P, P], FP32)
        ones = sb("ones", [P, P], BF16)
        earlier = sb("earlier", [P, P], BF16)
        not_earlier = sb("not_earlier", [P, P], BF16)
        zeros = sb("zeros", [P, TILES], FP32)
        zeros_b = sb("zeros_b", [P, TILES], BF16)
        ones_row = sb("ones_row", [1, P], FP32)
        filled = sb("filled", [P, TILES], I32)
        units = sb("units", [P, TILES], FP32)
        upto = sb("upto", [P, TILES], FP32)
        base = sb("base", [P, TILES], FP32)
        unit_no = sb("unit_no", [P, UCOLS], I32)
        unit_tile = sb("unit_tile", [P, UCOLS], FP32)
        unit_word = sb("unit_word", [P, UCOLS], I32)
        who = sb("who", [P, MT], I32)
        who_f = sb("who_f", [P, 4, MT], FP32)
        who_i = sb("who_i", [P, 4, MT], I32)
        who_bias = sb("who_bias", [P, MT], FP32)
        who_emb = sb("who_emb", [P, MT, F], FP32)
        users_t = sb("users_t", [F + 1, MT, P], FP32)
        istage = sb("istage", [P, 2, 4 * F], FP32)

        psum = ctx.enter_context(nc.psum_tensor("psum", [P, 8, 512], FP32))
        counts = psum[:, 0, 0:TILES]
        running = psum[:, 1, 0:TILES]

        s_const = sem("s_const")
        s_blank = sem("s_blank")
        s_rows = sem("s_rows")
        s_cols = sem("s_cols")
        s_vals = sem("s_vals")
        s_emb = sem("s_emb")
        s_mini = sem("s_mini")
        s_x0 = sem("s_x0")
        s_dve = sem("s_dve")
        s_ready = sem("s_ready")
        s_fill = sem("s_fill")
        s_filled = sem("s_filled")
        s_hot = sem("s_hot")
        s_key = sem("s_key")
        s_hotused = sem("s_hotused")
        s_base = sem("s_base")
        s_oh = sem("s_oh")
        s_ranked = sem("s_ranked")
        s_read = sem("s_read")
        s_copy = sem("s_copy")
        s_conv = sem("s_conv")
        s_place = sem("s_place")
        s_scat = [sem(f"s_scat{h}") for h in range(2)]
        s_pace = sem("s_pace")
        s_dvepace = sem("s_dvepace")
        s_uword = sem("s_uword")
        s_umap = sem("s_umap")
        s_uoff = sem("s_uoff")
        s_table = sem("s_table")
        s_tot = sem("s_tot")
        s_clean = sem("s_clean")
        s_ring = [sem(f"s_ring{h}") for h in range(2)]
        s_g = [sem(f"s_g{c}") for c in range(RING)]
        s_spread = sem("s_spread")
        s_chunk = sem("s_chunk")
        s_add = sem("s_add")
        s_who = sem("s_who")
        s_whoidx = sem("s_whoidx")
        s_whobias = sem("s_whobias")
        s_fin = sem("s_fin")
        s_urows = sem("s_urows")
        s_uemb = sem("s_uemb")
        s_ut = sem("s_ut")
        s_utc = sem("s_utc")
        s_stage = sem("s_stage")
        s_it = sem("s_it")
        s_itc = sem("s_itc")
        s_bias = sem("s_bias")
        s_rate = sem("s_rate")
        s_sig = sem("s_sig")
        s_out = [sem(f"s_out{m}") for m in range(MT)]

        block = ctx.enter_context(nc.Block())

        @block.sync
        def _(sp):
            sp.wait_ge(s_blank, 1)
            sp.dma_start(rows_i[0:P - 1, :], rows[0:(P - 1) * T].rearrange("(p t) -> p t", t=T)).then_inc(s_rows, 16)
            sp.dma_start(rows_i[P - 1:P, 0:LAST_E], rows[(P - 1) * T:NNZ].rearrange("(p t) -> p t", p=1)).then_inc(s_rows, 16)
            sp.wait_ge(s_blank, 2)
            sp.dma_start(cols_i[0:P - 1, :], cols[0:(P - 1) * T].rearrange("(p t) -> p t", t=T)).then_inc(s_cols, 16)
            sp.dma_start(cols_i[P - 1:P, 0:LAST_E], cols[(P - 1) * T:NNZ].rearrange("(p t) -> p t", p=1)).then_inc(s_cols, 16)
            sp.wait_ge(s_fill, 2)
            for n in range(RING):
                w = 4 * (K // RING)
                sp.dma_start(slots_v[:, n * w:(n + 1) * w], fill_sb[:, :, :].rearrange("p k w -> p (k w)")).then_inc(s_filled, 16)
            sp.wait_ge(s_blank, 4)
            for dst, ue, ie, s in ((new3, emb_u, emb_i, s_emb), (mini[:, :, :], mm_u, mm_i, s_mini)):
                sp.dma_start(dst[:, 0:UTILES - 1, :], ue[0:(UTILES - 1) * P, :].rearrange("(t p) f -> p t f", p=P)).then_inc(s, 16)
                sp.dma_start(dst[0:U_LANES, UTILES - 1, :], ue[(UTILES - 1) * P:USERS, :]).then_inc(s, 16)
                sp.dma_start(dst[U_LANES:P, UTILES - 1, :], ie[0:I_FIRST, :]).then_inc(s, 16)
                sp.dma_start(dst[:, UTILES:UTILES + I_TILES, :], ie[I_FIRST:I_FIRST + I_TILES * P, :].rearrange("(t p) f -> p t f", p=P)).then_inc(s, 16)
                sp.dma_start(dst[0:I_LAST, TILES - 1, :], ie[I_FIRST + I_TILES * P:ITEMS, :]).then_inc(s, 16)
            sp.wait_ge(s_uword, 1)
            sp.dma_start(unit_map[:, :], unit_word[:, :]).then_inc(s_umap, 16)
            sp.wait_ge(s_umap, 16)
            sp.dma_start(unit_off[0:1, :], unit_map.rearrange("(o p) j -> o (p j)", o=1)).then_inc(s_uoff, 16)
            sp.wait_ge(s_x0, 1)
            for h in range(2):
                sp.wait_ge(s_scat[h], 16 * SG * SORT_ITERS)
            with sp.Fori(0, LAYERS) as layer:
                sp.wait_ge(s_add, layer * (K * UNITS) + UNITS * PS_SLOTS)
                sp.dma_start(table_v, new[:, :]).then_inc(s_table, 16)
                with sp.Fori(0, LAYER_ITERS) as i:
                    for h in range(2):
                        sp.wait_ge(s_chunk, (layer * LAYER_ITERS + i) * RING + (h + 1) * LG)
                        sp.dma_start(ring[:, h, :, :].rearrange("p c w -> p (c w)"),
                                     slots_v[:, bass.ds(i * (RING * 4) + h * LG * 4, LG * 4)]).then_inc(s_ring[h], 16)
            sp.wait_ge(s_fin, 1)
            sp.dma_start(user_rows.rearrange("(p t) f -> p (t f)", p=P), total[:, 0:UTILES * F]).then_inc(s_urows, 16)
            sp.dma_start(items_t[F:F + 1, :], bias_i.rearrange("(o n) -> o n", o=1)).then_inc(s_bias, 16)
            with sp.Fori(0, ITEMS // NB) as j:
                for m in range(MT):
                    sp.wait_ge(s_sig, j * MT + (MT + m + 1))
                    sp.dma_start(out_v[:, m, bass.ds(j * NB, NB)], rated[:, m, :]).then_inc(s_out[m], 16)
            for m in range(MT):
                sp.wait_ge(s_out[m], 16 * (ITEMS // NB))

        @block.scalar
        def _(act):
            act.wait_ge(s_blank, 3)
            act.dma_start(vals_f[0:P - 1, :], vals[0:(P - 1) * T].rearrange("(p t) -> p t", t=T)).then_inc(s_vals, 16)
            act.dma_start(vals_f[P - 1:P, 0:LAST_E], vals[(P - 1) * T:NNZ].rearrange("(p t) -> p t", p=1)).then_inc(s_vals, 16)
            act.dma_start(who[:, :], users.rearrange("(p m) -> p m", m=MT)).then_inc(s_who, 16)
            act.wait_ge(s_fin, 1)
            for n in range(I_TILES // 4):
                if n >= 2:
                    act.wait_ge(s_it, n - 1)
                a = (UTILES + 4 * n) * F
                nc.scalar.activation(istage[:, n % 2, :], total[:, a:a + 4 * F], ACT.Copy).then_inc(s_stage, 1)
            act.wait_ge(s_whobias, 16 * MT)
            act.sem_inc(s_sig, MT)

            def rate(j, first):
                for m in range(MT):
                    act.wait_ge(s_rate, j * MT + (m + 1))
                    if not first:
                        act.wait_ge(s_out[m], j * 16)
                    nc.scalar.activation(rated[:, m, :], psum[:, m, 0:NB], ACT.Sigmoid,
                                         bias=who_bias[:, m:m + 1]).then_inc(s_sig, 1)

            rate(0, True)
            with act.Fori(1, ITEMS // NB) as j:
                rate(j, False)

        @block.gpsimd
        def _(pool):
            pool.iota(iota_i[:, :], pattern=[[1, TILES]], base=0, channel_multiplier=0).then_inc(s_const, 1)
            pool.iota(lane_i[:, :], pattern=[[1, 1]], base=0, channel_multiplier=1).then_inc(s_const, 1)
            pool.iota(unit_no[:, :], pattern=[[1, UCOLS]], base=0, channel_multiplier=UCOLS).then_inc(s_const, 1)
            pool.memset(fill_sb[:, :, 1:4], 0).then_inc(s_fill, 1)
            pool.memset(fill_sb[:, :, 0:1], ZERO_ROW).then_inc(s_fill, 1)
            pool.wait_ge(s_emb, 16 * 5)
            pool.wait_ge(s_mini, 16 * 5)
            new4 = new[:, :].rearrange("p (t r) -> p t r", r=F // MINI)
            small = mini[:, :, :].rearrange("p t (f o) -> p (t f) o", o=1).broadcast_to([P, TILES * MINI, F // MINI])
            pool.tensor_tensor(new4, new4, small, ALU.add).then_inc(s_x0, 1)
            pool.wait_ge(s_filled, 16 * RING)
            with pool.Fori(0, SORT_ITERS) as i:
                for h in range(2):
                    pool.wait_ge(s_place, i * 2 + (h + 1))
                    pool.sem_inc(s_pace, 1)
                    for c in range(SG):
                        pool.indirect_dma_start(
                            out=slots[:, :], out_offset=bass.IndirectOffsetOnAxis(ap=place[:, h, c:c + 1], axis=0),
                            in_=pay[:, h, c, :], in_offset=None).then_inc(s_scat[h], 16)
            with pool.Fori(0, LAYERS) as layer:
                pool.wait_ge(s_table, layer * 16 + 16)
                pool.sem_inc(s_pace, 1)
                with pool.Fori(0, LAYER_ITERS) as i:
                    for h in range(2):
                        pool.wait_ge(s_chunk, (layer * LAYER_ITERS + i) * RING + (h + 1) * LG)
                        pool.sem_inc(s_pace, 1)
                        pool.wait_ge(s_ring[h], (layer * LAYER_ITERS + i) * 16 + 16)
                        pool.sem_inc(s_pace, 1)
                        for c in range(LG):
                            pool.indirect_dma_start(
                                out=gathered[:, h * LG + c, :], out_offset=None, in_=table[:, :],
                                in_offset=bass.IndirectOffsetOnAxis(ap=ring[:, h, c, 0:1], axis=0)).then_inc(s_g[h * LG + c], 16)
            pool.wait_ge(s_whoidx, 1)
            for m in range(MT):
                pool.indirect_dma_start(
                    out=who_bias[:, m:m + 1], out_offset=None, in_=bias_u[:, :],
                    in_offset=bass.IndirectOffsetOnAxis(ap=who_i[:, 0, m:m + 1], axis=0)).then_inc(s_whobias, 16)
            pool.wait_ge(s_urows, 16)
            for m in range(MT):
                pool.indirect_dma_start(
                    out=who_emb[:, m, :], out_offset=None, in_=user_rows[:, :],
                    in_offset=bass.IndirectOffsetOnAxis(ap=who_i[:, 3, m:m + 1], axis=0)).then_inc(s_uemb, 16)

        @block.vector
        def _(dve):
            chain = [0]

            def link(ins):
                chain[0] += 1
                ins.then_inc(s_dve, 1)
                dve.wait_ge(s_dve, chain[0])

            nc.vector.memset(rows_i[96:P, LAST_E:T], ZERO_ROW).then_inc(s_blank, 1)
            nc.vector.memset(cols_i[96:P, LAST_E:T], ZERO_ROW).then_inc(s_blank, 1)
            nc.vector.memset(vals_f[96:P, LAST_E:T], 0.0).then_inc(s_blank, 1)
            nc.vector.memset(new3[:, TILES - 1, :], 0.0)
            nc.vector.memset(mini[:, TILES - 1, :], 0.0)
            link(nc.vector.memset(ones_row[:, :], 1.0))
            dve.sem_inc(s_blank, 1)
            nc.vector.memset(ones[:, :], 1.0)
            nc.vector.memset(zeros[:, :], 0.0)
            nc.vector.memset(zeros_b[:, :], 0.0)
            nc.vector.memset(users_t[F:F + 1, :, :], 1.0)
            dve.wait_ge(s_const, 3)
            nc.vector.tensor_copy(lane_f[:, :], lane_i[:, :])
            nc.vector.tensor_copy(iota_t[:, :], iota_i[:, :])
            link(nc.vector.tensor_copy(iota_l[:, :], iota_i[:, 0:P]))
            nc.vector.tensor_scalar(ident[:, :], iota_l[:, :], lane_f[:, 0:1], None, ALU.is_equal)
            nc.vector.tensor_scalar(earlier[:, :], iota_l[:, :], lane_f[:, 0:1], None, ALU.is_gt)
            nc.vector.tensor_scalar(not_earlier[:, :], iota_l[:, :], lane_f[:, 0:1], None, ALU.is_le).then_inc(s_ready, 1)

            dve.wait_ge(s_rows, 32)
            link(nc.vector.tensor_scalar(bits, rows_i, 7, None, ALU.logical_shift_right))
            link(nc.vector.tensor_copy(payload[:, :, 3], bits))

            def hot_group(i, h, first):
                if not first:
                    dve.wait_ge(s_hotused, i * 2 + (h - 1))
                nc.vector.tensor_copy(keys[:, h, :], payload[:, bass.ds(i * (2 * SG) + h * SG, SG), 3]).then_inc(s_key, 1)
                dve.wait_ge(s_key, i * 2 + (h + 1))
                for c in range(SG):
                    last = nc.vector.tensor_scalar(onehot[:, h * SG + c, :], iota_t[:, :], keys[:, h, c:c + 1],
                                                   None, ALU.is_equal)
                last.then_inc(s_hot, 1)

            for h in range(2):
                hot_group(0, h, True)
            with dve.Fori(1, SORT_ITERS) as i:
                for h in range(2):
                    hot_group(i, h, False)

            dve.wait_ge(s_vals, 32)
            nc.vector.tensor_copy(payload[:, :, 1], vals_f)
            link(nc.vector.tensor_scalar(bits, rows_i, P - 1, None, ALU.bitwise_and))
            link(nc.vector.tensor_copy(payload[:, :, 2], bits))
            dve.wait_ge(s_cols, 32)
            nc.vector.tensor_scalar(bits, cols_i, 7, None, ALU.logical_shift_right)
            link(nc.vector.tensor_scalar(rows_i, cols_i, P - 1, None, ALU.bitwise_and))
            link(nc.vector.scalar_tensor_tensor(payload_i[:, :, 0], rows_i, float(TILES), bits, ALU.mult, ALU.add))

            dve.wait_ge(s_hotused, 2 * SORT_ITERS)
            link(nc.vector.tensor_scalar(filled[:, :], counts, float(UNIT - 1), None, ALU.add))
            link(nc.vector.tensor_scalar(filled[:, :], filled[:, :], UNIT.bit_length() - 1, None, ALU.logical_shift_right))
            link(nc.vector.tensor_copy(units[:, :], filled[:, :]))
            link(nc.vector.tensor_tensor_scan(upto[:, :], units[:, :], zeros[:, :], 0.0, ALU.add, ALU.add))
            link(nc.vector.tensor_tensor(base[:, :], upto[:, :], units[:, :], ALU.subtract))
            nc.vector.tensor_scalar(base[:, :], base[:, :], float(UNIT), None, ALU.mult).then_inc(s_base, 1)

            def hot(h, c):
                nc.vector.tensor_scalar(onehot[:, c, :], iota_t[:, :], pay_f[:, h, c, 3:4], None,
                                        ALU.is_equal).then_inc(s_oh, 1)

            def rank_group(i, h, first):
                if not first:
                    dve.wait_ge(s_scat[h], i * (16 * SG))
                nc.vector.tensor_copy(pay[:, h, :, :], payload_i[:, bass.ds(i * (2 * SG) + h * SG, SG), :]).then_inc(s_copy, 1)
                dve.wait_ge(s_copy, i * 2 + (h + 1))
                hot(h, 0)
                for c in range(SG):
                    if c + 1 < SG:
                        hot(h, c + 1)
                    dve.wait_ge(s_ranked, i * (2 * SG) + (h * SG + c + 1))
                    nc.vector.tensor_tensor_reduce(
                        out=picked[:, :], in0=running, in1=onehot[:, c, :], scale=1.0, scalar=0.0,
                        op0=ALU.mult, op1=ALU.add, accum_out=rank[:, h, c:c + 1]).then_inc(s_read, 1)
                dve.wait_ge(s_read, i * (2 * SG) + (h + 1) * SG)
                nc.vector.tensor_copy(rank_i[:, :], rank[:, h, :]).then_inc(s_conv, 1)
                dve.wait_ge(s_conv, (i * 2 + h) * 2 + 1)
                nc.vector.tensor_scalar(rank_lo[:, :], rank_i[:, :], P - 1, None, ALU.bitwise_and)
                nc.vector.tensor_scalar(rank_hi[:, :], rank_i[:, :], 7, None, ALU.logical_shift_right).then_inc(s_conv, 1)
                dve.wait_ge(s_conv, (i * 2 + h) * 2 + 2)
                nc.vector.scalar_tensor_tensor(place[:, h, :], rank_lo[:, :], float(K), rank_hi[:, :],
                                               ALU.mult, ALU.add).then_inc(s_place, 1)

            for h in range(2):
                rank_group(0, h, True)
            with dve.Fori(1, SORT_ITERS) as i:
                for h in range(2):
                    rank_group(i, h, False)

            n_b = unit_no[:, :].rearrange("p (j o) -> p j o", o=1).broadcast_to([P, UCOLS, TILES])
            u_b = upto[:, :].rearrange("p (o t) -> p o t", o=1).broadcast_to([P, UCOLS, TILES])
            link(nc.vector.tensor_tensor(below, u_b, n_b, ALU.is_le))
            link(nc.vector.tensor_reduce(unit_tile[:, :], below, AX.X, ALU.add))
            nc.vector.tensor_scalar(unit_word[:, :], unit_tile[:, :], float(TILES - 1), float(F),
                                    ALU.min, ALU.mult).then_inc(s_uword, 1)

            dve.wait_ge(s_who, 16)
            link(nc.vector.tensor_copy(who_f[:, 0, :], who[:, :]))
            link(nc.vector.tensor_scalar(who_f[:, 1, :], who_f[:, 0, :], 0.0, float(USERS), ALU.is_lt, ALU.mult))
            link(nc.vector.tensor_tensor(who_f[:, 2, :], who_f[:, 0, :], who_f[:, 1, :], ALU.add))
            link(nc.vector.tensor_scalar(who_i[:, 0, :], who_f[:, 2, :], 0.0, float(USERS - 1), ALU.max, ALU.min))
            nc.vector.tensor_scalar(who_i[:, 1, :], who_i[:, 0, :], P - 1, None, ALU.bitwise_and)
            link(nc.vector.tensor_scalar(who_i[:, 2, :], who_i[:, 0, :], 7, None, ALU.logical_shift_right))
            nc.vector.scalar_tensor_tensor(who_i[:, 3, :], who_i[:, 1, :], float(UTILES), who_i[:, 2, :],
                                           ALU.mult, ALU.add).then_inc(s_whoidx, 1)

            dve.wait_ge(s_x0, 1)
            nc.vector.tensor_copy(total[:, :], new[:, :]).then_inc(s_tot, 1)
            dve.wait_ge(s_uoff, 16)
            dve.sem_inc(s_add, UNITS * PS_SLOTS)

            with dve.Fori(0, LAYERS) as layer:
                dve.wait_ge(s_table, layer * 16 + 16)
                dve.wait_ge(s_tot, layer + 1)
                nc.vector.memset(new[:, :], 0.0).then_inc(s_clean, 1)
                dve.wait_ge(s_clean, layer + 1)
                dve.sem_inc(s_dvepace, 1)
                with dve.Fori(0, LAYER_ITERS) as i:
                    done = (layer * LAYER_ITERS + i) * RING

                    def values(h, c):
                        n = h * LG + c
                        dve.wait_ge(s_chunk, done + (RING - R_SLOTS + n + 1))
                        nc.vector.tensor_scalar(spread[:, n % R_SLOTS, :], iota_l[:, :], ring_f[:, h, c, 2:3],
                                                ring_f[:, h, c, 1:2], ALU.is_equal, ALU.mult).then_inc(s_spread, 1)

                    for h in range(2):
                        dve.wait_ge(s_ring[h], (layer * LAYER_ITERS + i) * 16 + 16)
                        _, at = nc.values_load_multi_w_load_instructions(
                            unit_off[0:1, bass.ds(i * (RING * UNITS) + h * LG * UNITS, LG * UNITS)],
                            engines=(mybir.EngineType.DVE,), min_val=0, max_val=(TILES - 1) * F,
                            skip_runtime_bounds_check_because="the chip clamps each to (TILES - 1) * F above")
                        values(h, 0)
                        values(h, 1)
                        for c in range(LG):
                            n = h * LG + c
                            if c + 2 < LG:
                                values(h, c + 2)
                            dve.wait_ge(s_chunk, done + (RING + n + 1))
                            for u in range(UNITS):
                                dve.wait_ge(s_add, done * UNITS + (UNITS * (PS_SLOTS + n) + u))
                                tile = new[:, bass.ds(at[c * UNITS + u], F)]
                                nc.vector.tensor_tensor(tile, tile, psum[:, (n % PS_SLOTS) * UNITS + u, 0:F],
                                                        ALU.add).then_inc(s_add, 1)
                dve.wait_ge(s_add, (layer + 1) * (K * UNITS) + UNITS * PS_SLOTS)
                nc.vector.tensor_tensor(total[:, :], total[:, :], new[:, :], ALU.add).then_inc(s_tot, 1)

            dve.wait_ge(s_tot, LAYERS + 1)
            nc.vector.tensor_scalar(total[:, :], total[:, :], 1.0 / (LAYERS + 1), None, ALU.mult).then_inc(s_fin, 1)
            for n in range(I_TILES // 4):
                dve.wait_ge(s_it, n + 1)
                a = I_FIRST + 4 * P * n
                nc.vector.tensor_copy(items_t[0:F, a:a + 4 * P], psum[0:F, n % 2, :]).then_inc(s_itc, 1)
            dve.wait_ge(s_it, I_TILES // 4 + 1)
            nc.vector.tensor_copy(items_t[0:F, 0:I_FIRST], psum[0:F, 2, U_LANES:P])
            a = ITEMS - I_LAST - P
            nc.vector.tensor_copy(items_t[0:F, a:ITEMS], psum[0:F, 2, P:2 * P + I_LAST]).then_inc(s_itc, 1)
            for m in range(MT):
                dve.wait_ge(s_ut, m + 1)
                nc.vector.tensor_copy(users_t[0:F, m, :], psum[0:F, 3 + m % 2, 0:P]).then_inc(s_utc, 1)

        @block.tensor
        def _(pe):
            pe.sem_inc(s_chunk, RING)
            pe.wait_ge(s_ready, 1)
            pe.matmul(counts, ones[:, :], zeros_b[:, :], start=True, stop=True, skip_group_check=True)
            with pe.Fori(0, SORT_ITERS) as i:
                for h in range(2):
                    pe.wait_ge(s_hot, i * 2 + (h + 1))
                    for c in range(SG):
                        last = pe.matmul(counts, ones[:, :], onehot[:, h * SG + c, :], start=False, stop=True, skip_group_check=True)
                    last.then_inc(s_hotused, 1)
            pe.wait_ge(s_base, 1)
            pe.matmul(running, ones_row[:, :], base[0:1, :], start=True, stop=True, skip_group_check=True)
            with pe.Fori(0, SORT_ITERS) as i:
                for h in range(2):
                    for c in range(SG):
                        n = h * SG + c + 1
                        pe.wait_ge(s_oh, i * (2 * SG) + n)
                        pe.matmul(running, earlier[:, :], onehot[:, c, :], start=False, stop=True, skip_group_check=True).then_inc(s_ranked, 1)
                        pe.wait_ge(s_read, i * (2 * SG) + n)
                        pe.matmul(running, not_earlier[:, :], onehot[:, c, :], start=False, stop=True, skip_group_check=True)
            with pe.Fori(0, LAYERS) as layer:
                with pe.Fori(0, LAYER_ITERS) as i:
                    done = (layer * LAYER_ITERS + i) * RING
                    for n in range(RING):
                        pe.wait_ge(s_spread, done + (n + 1))
                        pe.wait_ge(s_g[n], (layer * LAYER_ITERS + i) * 16 + 16)
                        pe.wait_ge(s_add, done * UNITS + UNITS * (n + 1))
                        for u in range(UNITS):
                            a, b = u * UNIT, (u + 1) * UNIT
                            last = pe.matmul(psum[:, (n % PS_SLOTS) * UNITS + u, 0:F], spread[a:b, n % R_SLOTS, :],
                                             gathered[a:b, n, :], start=True, stop=True)
                        last.then_inc(s_chunk, 1)
            pe.wait_ge(s_fin, 1)
            for n in range(I_TILES // 4):
                pe.wait_ge(s_stage, n + 1)
                if n >= 2:
                    pe.wait_ge(s_itc, n - 1)
                for q in range(4):
                    last = pe.transpose(psum[0:F, n % 2, q * P:(q + 1) * P], istage[:, n % 2, q * F:(q + 1) * F], ident[:, :])
                last.then_inc(s_it, 1)
            for q, t in enumerate((UTILES - 1, TILES - 2, TILES - 1)):
                last = pe.transpose(psum[0:F, 2, q * P:(q + 1) * P], total[:, t * F:(t + 1) * F], ident[:, :])
            last.then_inc(s_it, 1)
            pe.wait_ge(s_uemb, 16 * MT)
            for m in range(MT):
                if m >= 2:
                    pe.wait_ge(s_utc, m - 1)
                pe.transpose(psum[0:F, 3 + m % 2, 0:P], who_emb[:, m, :], ident[:, :]).then_inc(s_ut, 1)
            pe.wait_ge(s_itc, I_TILES // 4 + 1)
            pe.wait_ge(s_utc, MT)
            pe.wait_ge(s_bias, 16)
            with pe.Fori(0, ITEMS // NB) as j:
                for m in range(MT):
                    pe.wait_ge(s_sig, j * MT + (m + 1))
                    pe.matmul(psum[:, m, 0:NB], users_t[:, m, :], items_t[:, bass.ds(j * NB, NB)], start=True, stop=True).then_inc(s_rate, 1)


_INS = ["r_users", "L0_rec_emb_user", "L0_rec_emb_item", "L0_rec_bias_user", "L0_rec_bias_item",
        "L0_rec_mm_emb_user", "L0_rec_mm_emb_item", "L0_rec_graph_vals", "L0_rec_graph_rows",
        "L0_rec_graph_cols"]


def kernel(**inputs):
    import numpy as _np
    import concourse.bacc as _bacc
    from concourse import mybir as _mybir
    from concourse.bass_utils import run_bass_kernel_spmd as _run

    nc = _bacc.Bacc("TRN2", target_bir_lowering=False, num_devices=1)
    arrays, args = {}, []
    for name in _INS:
        a = _np.ascontiguousarray(inputs[name])
        if name == "L0_rec_bias_item":
            a = a.reshape(-1)
        arrays[name] = a
        args.append(nc.dram_tensor(name, a.shape, _mybir.dt.from_np(a.dtype), kind="ExternalInput").ap())
    args.append(nc.dram_tensor("out", (BATCH, ITEMS), _mybir.dt.float32, kind="ExternalOutput").ap())
    build(nc, *args)
    r = _run(nc, [arrays], core_ids=[0])
    return r.results[0]["out"]
```

```python
from contextlib import ExitStack

import concourse.bass as bass
from concourse import mybir

FP32 = mybir.dt.float32
BF16 = mybir.dt.bfloat16
I32 = mybir.dt.int32
ALU = mybir.AluOpType
ACT = mybir.ActivationFunctionType
AX = mybir.AxisListType

P = 128
USERS, ITEMS, F, MINI = 6250, 12500, 64, 16
NODES = USERS + ITEMS
NNZ = 250000
BATCH = 1024
LAYERS = 3
TILES = -(-NODES // P)
TABLE = TILES * P
ZERO_ROW = TABLE - 1

TW = TILES + TILES % 2
SG = 14
SORT_ITERS = -(-NNZ // (P * 2 * SG))
T = SORT_ITERS * 2 * SG
EDGES = T * P
LAST_E = NNZ - (P - 1) * T

UNITS = 2
UNIT = P // UNITS
LG = 8
RING = 2 * LG
K_LEAST = -(-(EDGES + TILES * (UNIT - 1)) // P)
LAYER_ITERS = -(-K_LEAST // RING)
K = LAYER_ITERS * RING
UCOLS = -(-K * UNITS // P)
R_SLOTS = 8
AHEAD = 4
PS_SLOTS = 4
UTILES = -(-USERS // P)
U_LANES = USERS - (UTILES - 1) * P
I_FIRST = UTILES * P - USERS
I_TILES = (NODES // P) - UTILES
I_LAST = NODES - (NODES // P) * P
NB = 500
MT = BATCH // P


def build(nc, users, emb_u, emb_i, bias_u, bias_i, mm_u, mm_i, vals, rows, cols, out):
    table = nc.dram_tensor("table", [TABLE, F], FP32)
    slots = nc.dram_tensor("slots", [P * K, 4], I32)
    unit_map = nc.dram_tensor("unit_map", [P, UCOLS], I32)
    user_rows = nc.dram_tensor("user_rows", [P * UTILES, F], FP32)
    table_v = table.rearrange("(p t) f -> p (t f)", p=P)
    slots_v = slots.rearrange("(p k) w -> p (k w)", p=P)
    out_v = out.rearrange("(p m) n -> p m n", m=MT)

    with ExitStack() as ctx:
        def sb(name, shape, dt):
            return ctx.enter_context(nc.sbuf_tensor(name, shape, dt))

        def sem(name):
            return ctx.enter_context(nc.semaphore(name))

        arena = sb("arena", [P, ITEMS], FP32)
        payload = arena[:, 0:4 * T].rearrange("p (t w) -> p t w", w=4)
        payload_i = payload.bitcast(I32)
        rows_i = arena[:, 4 * T:5 * T].bitcast(I32)
        cols_i = arena[:, 5 * T:6 * T].bitcast(I32)
        resident = arena[:, 0:4 * (K + RING)].bitcast(I32).rearrange("p (k w) -> p k w", w=4)
        below = arena[:, 4 * (K + RING):ITEMS].bitcast(BF16)[:, 0:UCOLS * TILES].rearrange(
            "p (j t) -> p j t", t=TILES)
        items_t = arena[0:F + 1, :]
        rated = sb("rated", [P, MT, NB], FP32)
        flat = rated[:, :, :].rearrange("p m n -> p (m n)")
        vals_f = flat[:, 0:T]
        bits = flat[:, T:2 * T].bitcast(I32)
        new = sb("new", [P, TILES * F], FP32)
        total = sb("total", [P, TILES * F], FP32)
        new3 = new[:, :].rearrange("p (t f) -> p t f", f=F)
        mini = sb("mini", [P, TILES, MINI], FP32)
        fill_sb = sb("fill_sb", [P, K // RING, 4], I32)
        unit_off = sb("unit_off", [1, P * UCOLS], I32)
        gathered = sb("gathered", [P, RING, F], FP32)
        spread = sb("spread", [P, R_SLOTS, P], FP32)
        ring = sb("ring", [P, 2, LG, 4], I32)
        ring_f = ring[:, :, :, :].bitcast(FP32)
        pay = sb("pay", [P, 2, SG, 4], I32)
        pay_f = pay[:, :, :, :].bitcast(FP32)
        keys = sb("keys", [P, 2, SG], FP32)
        onehot = sb("onehot", [P, 2 * SG, TW], BF16)
        picked = sb("picked", [P, SG, TW], BF16)
        rank = sb("rank", [P, 2, SG], FP32)
        rank_i = sb("rank_i", [P, SG], I32)
        rank_lo = sb("rank_lo", [P, SG], I32)
        rank_hi = sb("rank_hi", [P, SG], I32)
        place = sb("place", [P, 2, SG], I32)
        iota_i = sb("iota_i", [P, TW], I32)
        lane_i = sb("lane_i", [P, 1], I32)
        lane_f = sb("lane_f", [P, 1], FP32)
        iota_t = sb("iota_t", [P, TW], BF16)
        iota_l = sb("iota_l", [P, P], FP32)
        ident = sb("ident", [P, P], FP32)
        ones = sb("ones", [P, P], BF16)
        earlier = sb("earlier", [P, P], BF16)
        not_earlier = sb("not_earlier", [P, P], BF16)
        zeros = sb("zeros", [P, TW], FP32)
        zeros_b = sb("zeros_b", [P, TW], BF16)
        ones_row = sb("ones_row", [1, P], FP32)
        filled = sb("filled", [P, TW], I32)
        units = sb("units", [P, TW], FP32)
        upto = sb("upto", [P, TW], FP32)
        base = sb("base", [P, 2, TW], FP32)
        unit_no = sb("unit_no", [P, UCOLS], I32)
        unit_tile = sb("unit_tile", [P, UCOLS], FP32)
        unit_word = sb("unit_word", [P, UCOLS], I32)
        who = sb("who", [P, MT], I32)
        who_f = sb("who_f", [P, 4, MT], FP32)
        who_i = sb("who_i", [P, 4, MT], I32)
        who_bias = sb("who_bias", [P, MT], FP32)
        who_emb = sb("who_emb", [P, MT, F], FP32)
        users_t = sb("users_t", [F + 1, MT, P], FP32)
        istage = sb("istage", [P, 2, 4 * F], FP32)

        psum = ctx.enter_context(nc.psum_tensor("psum", [P, 8, 512], FP32))
        counts = psum[:, 0, 0:TW]
        running = psum[:, 1, 0:2 * TW]

        s_const = sem("s_const")
        s_blank = sem("s_blank")
        s_rows = sem("s_rows")
        s_cols = sem("s_cols")
        s_vals = sem("s_vals")
        s_emb = sem("s_emb")
        s_mini = sem("s_mini")
        s_x0 = sem("s_x0")
        s_dve = sem("s_dve")
        s_ready = sem("s_ready")
        s_fill = sem("s_fill")
        s_filled = sem("s_filled")
        s_hot = sem("s_hot")
        s_key = sem("s_key")
        s_hotused = sem("s_hotused")
        s_base = sem("s_base")
        s_oh = sem("s_oh")
        s_ranked = sem("s_ranked")
        s_read = sem("s_read")
        s_copy = sem("s_copy")
        s_conv = sem("s_conv")
        s_place = sem("s_place")
        s_scat = [sem(f"s_scat{h}") for h in range(2)]
        s_pace = sem("s_pace")
        s_dvepace = sem("s_dvepace")
        s_uword = sem("s_uword")
        s_umap = sem("s_umap")
        s_uoff = sem("s_uoff")
        s_table = sem("s_table")
        s_tot = sem("s_tot")
        s_clean = sem("s_clean")
        s_head = sem("s_head")
        s_rest = sem("s_rest")
        s_pay = sem("s_pay")
        s_g = [sem(f"s_g{c}") for c in range(RING)]
        s_spread = sem("s_spread")
        s_chunk = sem("s_chunk")
        s_add = sem("s_add")
        s_who = sem("s_who")
        s_whoidx = sem("s_whoidx")
        s_whobias = sem("s_whobias")
        s_fin = sem("s_fin")
        s_urows = sem("s_urows")
        s_uemb = sem("s_uemb")
        s_ut = sem("s_ut")
        s_utc = sem("s_utc")
        s_stage = sem("s_stage")
        s_it = sem("s_it")
        s_itc = sem("s_itc")
        s_bias = sem("s_bias")
        s_rate = sem("s_rate")
        s_sig = sem("s_sig")
        s_out = [sem(f"s_out{m}") for m in range(MT)]

        block = ctx.enter_context(nc.Block())

        @block.sync
        def _(sp):
            sp.wait_ge(s_blank, 1)
            sp.dma_start(rows_i[0:P - 1, :], rows[0:(P - 1) * T].rearrange("(p t) -> p t", t=T)).then_inc(s_rows, 16)
            sp.dma_start(rows_i[P - 1:P, 0:LAST_E], rows[(P - 1) * T:NNZ].rearrange("(p t) -> p t", p=1)).then_inc(s_rows, 16)
            sp.wait_ge(s_blank, 2)
            sp.dma_start(cols_i[0:P - 1, :], cols[0:(P - 1) * T].rearrange("(p t) -> p t", t=T)).then_inc(s_cols, 16)
            sp.dma_start(cols_i[P - 1:P, 0:LAST_E], cols[(P - 1) * T:NNZ].rearrange("(p t) -> p t", p=1)).then_inc(s_cols, 16)
            sp.wait_ge(s_fill, 2)
            for n in range(RING):
                w = 4 * (K // RING)
                sp.dma_start(slots_v[:, n * w:(n + 1) * w], fill_sb[:, :, :].rearrange("p k w -> p (k w)")).then_inc(s_filled, 16)
            sp.wait_ge(s_blank, 4)
            for dst, ue, ie, s in ((new3, emb_u, emb_i, s_emb), (mini[:, :, :], mm_u, mm_i, s_mini)):
                sp.dma_start(dst[:, 0:UTILES - 1, :], ue[0:(UTILES - 1) * P, :].rearrange("(t p) f -> p t f", p=P)).then_inc(s, 16)
                sp.dma_start(dst[0:U_LANES, UTILES - 1, :], ue[(UTILES - 1) * P:USERS, :]).then_inc(s, 16)
                sp.dma_start(dst[U_LANES:P, UTILES - 1, :], ie[0:I_FIRST, :]).then_inc(s, 16)
                sp.dma_start(dst[:, UTILES:UTILES + I_TILES, :], ie[I_FIRST:I_FIRST + I_TILES * P, :].rearrange("(t p) f -> p t f", p=P)).then_inc(s, 16)
                sp.dma_start(dst[0:I_LAST, TILES - 1, :], ie[I_FIRST + I_TILES * P:ITEMS, :]).then_inc(s, 16)
            sp.wait_ge(s_x0, 1)
            sp.dma_start(table_v, new[:, :]).then_inc(s_table, 16)
            sp.wait_ge(s_uword, 1)
            sp.dma_start(unit_map[:, :], unit_word[:, :]).then_inc(s_umap, 16)
            sp.wait_ge(s_umap, 16)
            sp.dma_start(unit_off[0:1, :], unit_map.rearrange("(o p) j -> o (p j)", o=1)).then_inc(s_uoff, 16)
            for h in range(2):
                sp.wait_ge(s_scat[h], 16 * SG * SORT_ITERS)
            res = arena[:, 0:4 * (K + RING)].bitcast(I32)
            sp.dma_start(res[:, 0:4 * RING], slots_v[:, 0:4 * RING]).then_inc(s_head, 16)
            sp.dma_start(res[:, 4 * RING:4 * K], slots_v[:, 4 * RING:4 * K]).then_inc(s_rest, 16)
            sp.dma_start(res[:, 4 * K:4 * (K + RING)], slots_v[:, 0:4 * RING]).then_inc(s_rest, 16)
            with sp.Fori(1, LAYERS) as layer:
                sp.wait_ge(s_add, layer * (K * UNITS) + UNITS * PS_SLOTS)
                sp.dma_start(table_v, new[:, :]).then_inc(s_table, 16)
            sp.wait_ge(s_fin, 1)
            sp.dma_start(user_rows.rearrange("(p t) f -> p (t f)", p=P), total[:, 0:UTILES * F]).then_inc(s_urows, 16)
            sp.dma_start(items_t[F:F + 1, :], bias_i.rearrange("(o n) -> o n", o=1)).then_inc(s_bias, 16)
            with sp.Fori(0, ITEMS // NB) as j:
                for m in range(MT):
                    sp.wait_ge(s_sig, j * MT + (MT + m + 1))
                    sp.dma_start(out_v[:, m, bass.ds(j * NB, NB)], rated[:, m, :]).then_inc(s_out[m], 16)
            for m in range(MT):
                sp.wait_ge(s_out[m], 16 * (ITEMS // NB))

        @block.scalar
        def _(act):
            act.wait_ge(s_blank, 3)
            act.dma_start(vals_f[0:P - 1, :], vals[0:(P - 1) * T].rearrange("(p t) -> p t", t=T)).then_inc(s_vals, 16)
            act.dma_start(vals_f[P - 1:P, 0:LAST_E], vals[(P - 1) * T:NNZ].rearrange("(p t) -> p t", p=1)).then_inc(s_vals, 16)
            act.dma_start(who[:, :], users.rearrange("(p m) -> p m", m=MT)).then_inc(s_who, 16)
            act.wait_ge(s_fin, 1)
            for n in range(I_TILES // 4):
                if n >= 2:
                    act.wait_ge(s_it, n - 1)
                a = (UTILES + 4 * n) * F
                nc.scalar.activation(istage[:, n % 2, :], total[:, a:a + 4 * F], ACT.Copy).then_inc(s_stage, 1)
            act.wait_ge(s_whobias, 16 * MT)
            act.sem_inc(s_sig, MT)

            def rate(j, first):
                for m in range(MT):
                    act.wait_ge(s_rate, j * MT + (m + 1))
                    if not first:
                        act.wait_ge(s_out[m], j * 16)
                    nc.scalar.activation(rated[:, m, :], psum[:, m, 0:NB], ACT.Sigmoid,
                                         bias=who_bias[:, m:m + 1]).then_inc(s_sig, 1)

            rate(0, True)
            with act.Fori(1, ITEMS // NB) as j:
                rate(j, False)

        @block.gpsimd
        def _(pool):
            pool.iota(iota_i[:, :], pattern=[[1, TW]], base=0, channel_multiplier=0).then_inc(s_const, 1)
            pool.iota(lane_i[:, :], pattern=[[1, 1]], base=0, channel_multiplier=1).then_inc(s_const, 1)
            pool.iota(unit_no[:, :], pattern=[[1, UCOLS]], base=0, channel_multiplier=UCOLS).then_inc(s_const, 1)
            pool.memset(fill_sb[:, :, 1:4], 0).then_inc(s_fill, 1)
            pool.memset(fill_sb[:, :, 0:1], ZERO_ROW).then_inc(s_fill, 1)
            pool.wait_ge(s_emb, 16 * 5)
            pool.wait_ge(s_mini, 16 * 5)
            new4 = new[:, :].rearrange("p (t r) -> p t r", r=F // MINI)
            small = mini[:, :, :].rearrange("p t (f o) -> p (t f) o", o=1).broadcast_to([P, TILES * MINI, F // MINI])
            pool.tensor_tensor(new4, new4, small, ALU.add).then_inc(s_x0, 1)
            pool.wait_ge(s_filled, 16 * RING)
            with pool.Fori(0, SORT_ITERS) as i:
                for h in range(2):
                    pool.wait_ge(s_place, i * 2 + (h + 1))
                    pool.sem_inc(s_pace, 1)
                    for c in range(SG):
                        pool.indirect_dma_start(
                            out=slots[:, :], out_offset=bass.IndirectOffsetOnAxis(ap=place[:, h, c:c + 1], axis=0),
                            in_=pay[:, h, c, :], in_offset=None).then_inc(s_scat[h], 16)
            with pool.Fori(0, LAYERS) as layer:
                pool.wait_ge(s_table, layer * 16 + 16)
                pool.sem_inc(s_pace, 1)
                with pool.Fori(0, LAYER_ITERS) as i:
                    for h in range(2):
                        pool.wait_ge(s_pay, (layer * LAYER_ITERS + i) * 2 + (h + 1))
                        pool.sem_inc(s_pace, 1)
                        for c in range(LG):
                            pool.indirect_dma_start(
                                out=gathered[:, h * LG + c, :], out_offset=None, in_=table[:, :],
                                in_offset=bass.IndirectOffsetOnAxis(ap=ring[:, h, c, 0:1], axis=0)).then_inc(s_g[h * LG + c], 16)
            pool.wait_ge(s_whoidx, 1)
            for m in range(MT):
                pool.indirect_dma_start(
                    out=who_bias[:, m:m + 1], out_offset=None, in_=bias_u[:, :],
                    in_offset=bass.IndirectOffsetOnAxis(ap=who_i[:, 0, m:m + 1], axis=0)).then_inc(s_whobias, 16)
            pool.wait_ge(s_urows, 16)
            for m in range(MT):
                pool.indirect_dma_start(
                    out=who_emb[:, m, :], out_offset=None, in_=user_rows[:, :],
                    in_offset=bass.IndirectOffsetOnAxis(ap=who_i[:, 3, m:m + 1], axis=0)).then_inc(s_uemb, 16)

        @block.vector
        def _(dve):
            chain = [0]

            def link(ins):
                chain[0] += 1
                ins.then_inc(s_dve, 1)
                dve.wait_ge(s_dve, chain[0])

            nc.vector.memset(rows_i[96:P, LAST_E:T], ZERO_ROW).then_inc(s_blank, 1)
            nc.vector.memset(cols_i[96:P, LAST_E:T], ZERO_ROW).then_inc(s_blank, 1)
            nc.vector.memset(vals_f[96:P, LAST_E:T], 0.0).then_inc(s_blank, 1)
            nc.vector.memset(new3[:, TILES - 1, :], 0.0)
            nc.vector.memset(mini[:, TILES - 1, :], 0.0)
            link(nc.vector.memset(ones_row[:, :], 1.0))
            dve.sem_inc(s_blank, 1)
            nc.vector.memset(ones[:, :], 1.0)
            nc.vector.memset(zeros[:, :], 0.0)
            nc.vector.memset(zeros_b[:, :], 0.0)
            nc.vector.memset(users_t[F:F + 1, :, :], 1.0)
            dve.wait_ge(s_const, 3)
            nc.vector.tensor_copy(lane_f[:, :], lane_i[:, :])
            nc.vector.tensor_copy(iota_t[:, :], iota_i[:, :])
            link(nc.vector.tensor_copy(iota_l[:, :], iota_i[:, 0:P]))
            nc.vector.tensor_scalar(ident[:, :], iota_l[:, :], lane_f[:, 0:1], None, ALU.is_equal)
            nc.vector.tensor_scalar(earlier[:, :], iota_l[:, :], lane_f[:, 0:1], None, ALU.is_gt)
            nc.vector.tensor_scalar(not_earlier[:, :], iota_l[:, :], lane_f[:, 0:1], None, ALU.is_le).then_inc(s_ready, 1)

            dve.wait_ge(s_rows, 32)
            link(nc.vector.tensor_scalar(bits, rows_i, 7, None, ALU.logical_shift_right))
            link(nc.vector.tensor_copy(payload[:, :, 3], bits))

            def hot_group(i, h, first):
                if not first:
                    dve.wait_ge(s_hotused, i * 2 + (h - 1))
                nc.vector.tensor_copy(keys[:, h, :], payload[:, bass.ds(i * (2 * SG) + h * SG, SG), 3]).then_inc(s_key, 1)
                dve.wait_ge(s_key, i * 2 + (h + 1))
                for c in range(SG):
                    last = nc.vector.tensor_scalar(onehot[:, h * SG + c, :], iota_t[:, :], keys[:, h, c:c + 1],
                                                   None, ALU.is_equal)
                last.then_inc(s_hot, 1)

            for h in range(2):
                hot_group(0, h, True)
            with dve.Fori(1, SORT_ITERS) as i:
                for h in range(2):
                    hot_group(i, h, False)

            dve.wait_ge(s_vals, 32)
            nc.vector.tensor_copy(payload[:, :, 1], vals_f)
            link(nc.vector.tensor_scalar(bits, rows_i, P - 1, None, ALU.bitwise_and))
            link(nc.vector.tensor_copy(payload[:, :, 2], bits))
            dve.wait_ge(s_cols, 32)
            nc.vector.tensor_scalar(bits, cols_i, 7, None, ALU.logical_shift_right)
            link(nc.vector.tensor_scalar(rows_i, cols_i, P - 1, None, ALU.bitwise_and))
            link(nc.vector.scalar_tensor_tensor(payload_i[:, :, 0], rows_i, float(TILES), bits, ALU.mult, ALU.add))

            dve.wait_ge(s_hotused, 2 * SORT_ITERS)
            link(nc.vector.tensor_scalar(filled[:, :], counts, float(UNIT - 1), None, ALU.add))
            link(nc.vector.tensor_scalar(filled[:, :], filled[:, :], UNIT.bit_length() - 1, None, ALU.logical_shift_right))
            link(nc.vector.tensor_copy(units[:, :], filled[:, :]))
            link(nc.vector.tensor_tensor_scan(upto[:, :], units[:, :], zeros[:, :], 0.0, ALU.add, ALU.add))
            link(nc.vector.tensor_tensor(base[:, 0, :], upto[:, :], units[:, :], ALU.subtract))
            nc.vector.tensor_scalar(base[:, 1, :], base[:, 0, :], float(UNIT), None, ALU.mult)
            nc.vector.tensor_scalar(base[:, 0, :], base[:, 0, :], float(UNIT), None, ALU.mult).then_inc(s_base, 1)

            def hot(h, c):
                nc.vector.tensor_scalar(onehot[:, c, :], iota_t[:, :], pay_f[:, h, c, 3:4], None,
                                        ALU.is_equal)
                nc.vector.tensor_scalar(onehot[:, c + 1, :], iota_t[:, :], pay_f[:, h, c + 1, 3:4], None,
                                        ALU.is_equal).then_inc(s_oh, 1)

            def rank_group(i, h, first):
                if not first:
                    dve.wait_ge(s_scat[h], i * (16 * SG))
                nc.vector.tensor_copy(pay[:, h, :, :], payload_i[:, bass.ds(i * (2 * SG) + h * SG, SG), :]).then_inc(s_copy, 1)
                dve.wait_ge(s_copy, i * 2 + (h + 1))
                hot(h, 0)
                for c in range(0, SG, 2):
                    if c + 2 < SG:
                        hot(h, c + 2)
                    dve.wait_ge(s_ranked, i * SG + (h * SG + c) // 2 + 1)
                    for e in range(2):
                        last = nc.vector.tensor_tensor_reduce(
                            out=picked[:, c + e, :], in0=running[:, e * TW:(e + 1) * TW], in1=onehot[:, c + e, :], scale=1.0,
                            scalar=0.0, op0=ALU.mult, op1=ALU.add, accum_out=rank[:, h, c + e:c + e + 1])
                    last.then_inc(s_read, 1)
                dve.wait_ge(s_read, i * SG + (h + 1) * SG // 2)
                nc.vector.tensor_copy(rank_i[:, :], rank[:, h, :]).then_inc(s_conv, 1)
                dve.wait_ge(s_conv, (i * 2 + h) * 2 + 1)
                nc.vector.tensor_scalar(rank_lo[:, :], rank_i[:, :], P - 1, None, ALU.bitwise_and)
                nc.vector.tensor_scalar(rank_hi[:, :], rank_i[:, :], 7, None, ALU.logical_shift_right).then_inc(s_conv, 1)
                dve.wait_ge(s_conv, (i * 2 + h) * 2 + 2)
                nc.vector.scalar_tensor_tensor(place[:, h, :], rank_lo[:, :], float(K), rank_hi[:, :],
                                               ALU.mult, ALU.add).then_inc(s_place, 1)

            for h in range(2):
                rank_group(0, h, True)
            with dve.Fori(1, SORT_ITERS) as i:
                for h in range(2):
                    rank_group(i, h, False)

            n_b = unit_no[:, :].rearrange("p (j o) -> p j o", o=1).broadcast_to([P, UCOLS, TILES])
            u_b = upto[:, 0:TILES].rearrange("p (o t) -> p o t", o=1).broadcast_to([P, UCOLS, TILES])
            link(nc.vector.tensor_tensor(below, u_b, n_b, ALU.is_le))
            link(nc.vector.tensor_reduce(unit_tile[:, :], below, AX.X, ALU.add))
            nc.vector.tensor_scalar(unit_word[:, :], unit_tile[:, :], float(TILES - 1), float(F),
                                    ALU.min, ALU.mult).then_inc(s_uword, 1)

            dve.wait_ge(s_who, 16)
            link(nc.vector.tensor_copy(who_f[:, 0, :], who[:, :]))
            link(nc.vector.tensor_scalar(who_f[:, 1, :], who_f[:, 0, :], 0.0, float(USERS), ALU.is_lt, ALU.mult))
            link(nc.vector.tensor_tensor(who_f[:, 2, :], who_f[:, 0, :], who_f[:, 1, :], ALU.add))
            link(nc.vector.tensor_scalar(who_i[:, 0, :], who_f[:, 2, :], 0.0, float(USERS - 1), ALU.max, ALU.min))
            nc.vector.tensor_scalar(who_i[:, 1, :], who_i[:, 0, :], P - 1, None, ALU.bitwise_and)
            link(nc.vector.tensor_scalar(who_i[:, 2, :], who_i[:, 0, :], 7, None, ALU.logical_shift_right))
            nc.vector.scalar_tensor_tensor(who_i[:, 3, :], who_i[:, 1, :], float(UTILES), who_i[:, 2, :],
                                           ALU.mult, ALU.add).then_inc(s_whoidx, 1)

            dve.wait_ge(s_x0, 1)
            nc.vector.tensor_copy(total[:, :], new[:, :]).then_inc(s_tot, 1)
            dve.sem_inc(s_add, UNITS * PS_SLOTS)
            dve.wait_ge(s_head, 16)
            for h in range(2):
                nc.vector.tensor_copy(ring[:, h, :, :], resident[:, h * LG:(h + 1) * LG, :]).then_inc(s_pay, 1)

            def values(n):
                h, c = n // LG % 2, n % LG
                nc.vector.tensor_scalar(spread[:, n % R_SLOTS, :], iota_l[:, :], ring_f[:, h, c, 2:3],
                                        ring_f[:, h, c, 1:2], ALU.is_equal, ALU.mult).then_inc(s_spread, 1)

            dve.wait_ge(s_pay, 1)
            for n in range(AHEAD):
                values(n)
            dve.wait_ge(s_rest, 32)
            dve.wait_ge(s_uoff, 16)

            with dve.Fori(0, LAYERS) as layer:
                dve.wait_ge(s_table, layer * 16 + 16)
                dve.wait_ge(s_tot, layer + 1)
                nc.vector.memset(new[:, :], 0.0).then_inc(s_clean, 1)
                dve.wait_ge(s_clean, layer + 1)
                dve.sem_inc(s_dvepace, 1)
                with dve.Fori(0, LAYER_ITERS) as i:
                    done = (layer * LAYER_ITERS + i) * RING

                    for h in range(2):
                        dve.wait_ge(s_pay, (layer * LAYER_ITERS + i) * 2 + (h + 2))
                        _, at = nc.values_load_multi_w_load_instructions(
                            unit_off[0:1, bass.ds(i * (RING * UNITS) + h * LG * UNITS, LG * UNITS)],
                            engines=(mybir.EngineType.DVE,), min_val=0, max_val=(TILES - 1) * F,
                            skip_runtime_bounds_check_because="the chip clamps each to (TILES - 1) * F above")
                        for c in range(0, LG, 2):
                            n = h * LG + c
                            dve.wait_ge(s_chunk, done + (n + 2))
                            for k in range(2 * UNITS):
                                dve.wait_ge(s_add, done * UNITS + (UNITS * (PS_SLOTS + n) + k))
                                tile = new[:, bass.ds(at[c * UNITS + k], F)]
                                nc.vector.tensor_tensor(tile, tile, psum[:, (n % PS_SLOTS) * UNITS + k, 0:F],
                                                        ALU.add).then_inc(s_add, 1)
                                if k < 2:
                                    values(n + AHEAD + k)
                        nc.vector.tensor_copy(ring[:, h, :, :], resident[:, bass.ds(i * RING + (RING + h * LG), LG), :]).then_inc(s_pay, 1)
                dve.wait_ge(s_add, (layer + 1) * (K * UNITS) + UNITS * PS_SLOTS)
                nc.vector.tensor_tensor(total[:, :], total[:, :], new[:, :], ALU.add).then_inc(s_tot, 1)

            dve.wait_ge(s_tot, LAYERS + 1)
            nc.vector.tensor_scalar(total[:, :], total[:, :], 1.0 / (LAYERS + 1), None, ALU.mult).then_inc(s_fin, 1)
            for n in range(I_TILES // 4):
                dve.wait_ge(s_it, n + 1)
                a = I_FIRST + 4 * P * n
                nc.vector.tensor_copy(items_t[0:F, a:a + 4 * P], psum[0:F, n % 2, :]).then_inc(s_itc, 1)
            dve.wait_ge(s_it, I_TILES // 4 + 1)
            nc.vector.tensor_copy(items_t[0:F, 0:I_FIRST], psum[0:F, 2, U_LANES:P])
            a = ITEMS - I_LAST - P
            nc.vector.tensor_copy(items_t[0:F, a:ITEMS], psum[0:F, 2, P:2 * P + I_LAST]).then_inc(s_itc, 1)
            for m in range(MT):
                dve.wait_ge(s_ut, m + 1)
                nc.vector.tensor_copy(users_t[0:F, m, :], psum[0:F, 3 + m % 2, 0:P]).then_inc(s_utc, 1)

        @block.tensor
        def _(pe):
            pe.wait_ge(s_ready, 1)
            pe.matmul(counts, ones[:, :], zeros_b[:, :], start=True, stop=True, skip_group_check=True)
            with pe.Fori(0, SORT_ITERS) as i:
                for h in range(2):
                    pe.wait_ge(s_hot, i * 2 + (h + 1))
                    for c in range(SG):
                        last = pe.matmul(counts, ones[:, :], onehot[:, h * SG + c, :], start=False, stop=True, skip_group_check=True)
                    last.then_inc(s_hotused, 1)
            pe.wait_ge(s_base, 1)
            pe.matmul(running, ones_row[:, :], base[0:1, :, :].rearrange("p a t -> p (a t)"), start=True, stop=True, skip_group_check=True)
            with pe.Fori(0, SORT_ITERS) as i:
                for h in range(2):
                    for c in range(0, SG, 2):
                        n = (h * SG + c) // 2 + 1
                        pair = onehot[:, c:c + 2, :].rearrange("p a t -> p (a t)")
                        pe.wait_ge(s_oh, i * SG + n)
                        pe.matmul(running, earlier[:, :], pair, start=False, stop=True, skip_group_check=True)
                        pe.matmul(running[:, TW:2 * TW], ones[:, :], onehot[:, c, :], start=False, stop=True, skip_group_check=True).then_inc(s_ranked, 1)
                        pe.wait_ge(s_read, i * SG + n)
                        pe.matmul(running, not_earlier[:, :], pair, start=False, stop=True, skip_group_check=True)
                        pe.matmul(running[:, 0:TW], ones[:, :], onehot[:, c + 1, :], start=False, stop=True, skip_group_check=True)
            with pe.Fori(0, LAYERS) as layer:
                with pe.Fori(0, LAYER_ITERS) as i:
                    done = (layer * LAYER_ITERS + i) * RING
                    for n in range(RING):
                        pe.wait_ge(s_spread, done + (n + 1))
                        pe.wait_ge(s_g[n], (layer * LAYER_ITERS + i) * 16 + 16)
                        pe.wait_ge(s_add, done * UNITS + UNITS * (n + 1))
                        for u in range(UNITS):
                            a, b = u * UNIT, (u + 1) * UNIT
                            last = pe.matmul(psum[:, (n % PS_SLOTS) * UNITS + u, 0:F], spread[a:b, n % R_SLOTS, :],
                                             gathered[a:b, n, :], start=True, stop=True)
                        last.then_inc(s_chunk, 1)
            pe.wait_ge(s_fin, 1)
            for n in range(I_TILES // 4):
                pe.wait_ge(s_stage, n + 1)
                if n >= 2:
                    pe.wait_ge(s_itc, n - 1)
                for q in range(4):
                    last = pe.transpose(psum[0:F, n % 2, q * P:(q + 1) * P], istage[:, n % 2, q * F:(q + 1) * F], ident[:, :])
                last.then_inc(s_it, 1)
            for q, t in enumerate((UTILES - 1, TILES - 2, TILES - 1)):
                last = pe.transpose(psum[0:F, 2, q * P:(q + 1) * P], total[:, t * F:(t + 1) * F], ident[:, :])
            last.then_inc(s_it, 1)
            pe.wait_ge(s_uemb, 16 * MT)
            for m in range(MT):
                if m >= 2:
                    pe.wait_ge(s_utc, m - 1)
                pe.transpose(psum[0:F, 3 + m % 2, 0:P], who_emb[:, m, :], ident[:, :]).then_inc(s_ut, 1)
            pe.wait_ge(s_itc, I_TILES // 4 + 1)
            pe.wait_ge(s_utc, MT)
            pe.wait_ge(s_bias, 16)
            with pe.Fori(0, ITEMS // NB) as j:
                for m in range(MT):
                    pe.wait_ge(s_sig, j * MT + (m + 1))
                    pe.matmul(psum[:, m, 0:NB], users_t[:, m, :], items_t[:, bass.ds(j * NB, NB)], start=True, stop=True).then_inc(s_rate, 1)


_INS = ["r_users", "L0_rec_emb_user", "L0_rec_emb_item", "L0_rec_bias_user", "L0_rec_bias_item",
        "L0_rec_mm_emb_user", "L0_rec_mm_emb_item", "L0_rec_graph_vals", "L0_rec_graph_rows",
        "L0_rec_graph_cols"]


def kernel(**inputs):
    import numpy as _np
    import concourse.bacc as _bacc
    from concourse import mybir as _mybir
    from concourse.bass_utils import run_bass_kernel_spmd as _run

    nc = _bacc.Bacc("TRN2", target_bir_lowering=False, num_devices=1)
    arrays, args = {}, []
    for name in _INS:
        a = _np.ascontiguousarray(inputs[name])
        if name == "L0_rec_bias_item":
            a = a.reshape(-1)
        arrays[name] = a
        args.append(nc.dram_tensor(name, a.shape, _mybir.dt.from_np(a.dtype), kind="ExternalInput").ap())
    args.append(nc.dram_tensor("out", (BATCH, ITEMS), _mybir.dt.float32, kind="ExternalOutput").ap())
    build(nc, *args)
    r = _run(nc, [arrays], core_ids=[0])
    return r.results[0]["out"]
```

```python
from contextlib import ExitStack

import concourse.bass as bass
from concourse import mybir

FP32 = mybir.dt.float32
BF16 = mybir.dt.bfloat16
I32 = mybir.dt.int32
ALU = mybir.AluOpType
ACT = mybir.ActivationFunctionType
AX = mybir.AxisListType

P = 128
USERS, ITEMS, F, MINI = 6250, 12500, 64, 16
NODES = USERS + ITEMS
NNZ = 250000
BATCH = 1024
LAYERS = 3
TILES = -(-NODES // P)
TABLE = TILES * P
ZERO_ROW = TABLE - 1

TW = TILES + TILES % 2
SG = 14
SORT_ITERS = -(-NNZ // (P * 2 * SG))
T = SORT_ITERS * 2 * SG
X0_TILES = 3
X0_ITERS = TILES // X0_TILES
assert X0_ITERS * X0_TILES == TILES and X0_ITERS + 1 < SORT_ITERS
EDGES = T * P
LAST_E = NNZ - (P - 1) * T

LOW = 16
HIGH = -(-TILES // LOW)
PACK = P // LOW
HG = 7 * PACK
HSLOTS = 5
HIST_ITERS = T // (HG * HSLOTS)
assert HIST_ITERS * HG * HSLOTS == T

UNITS = 2
UNIT = P // UNITS
LG = 8
RING = 2 * LG
K_LEAST = -(-(EDGES + (TILES - 1) * (UNIT - 1)) // P)
LAYER_ITERS = -(-K_LEAST // RING)
K = LAYER_ITERS * RING
UCOLS = -(-K * UNITS // P)
R_SLOTS = 8
AHEAD = 4
PS_SLOTS = 4
UTILES = -(-USERS // P)
U_LANES = USERS - (UTILES - 1) * P
I_FIRST = UTILES * P - USERS
I_TILES = (NODES // P) - UTILES
I_LAST = NODES - (NODES // P) * P
PIECES = [(UTILES, UTILES + 12), (UTILES + 12, TILES), (0, UTILES)]
TOT_DONE = LAYERS * len(PIECES) + 1
NB = 500
MT = BATCH // P


def build(nc, users, emb_u, emb_i, bias_u, bias_i, mm_u, mm_i, vals, rows, cols, out):
    table = nc.dram_tensor("table", [TABLE, F], FP32)
    slots = nc.dram_tensor("slots", [P * K, 4], I32)
    bias_parts = nc.dram_tensor("bias_parts", [3, ITEMS], BF16)
    unit_map = nc.dram_tensor("unit_map", [P, UCOLS], I32)
    user_rows = nc.dram_tensor("user_rows", [P * UTILES, F], FP32)
    table_v = table.rearrange("(p t) f -> p (t f)", p=P)
    slots_v = slots.rearrange("(p k) w -> p (k w)", p=P)
    out_v = out.rearrange("(p m) n -> p m n", m=MT)

    with ExitStack() as ctx:
        def sb(name, shape, dt):
            return ctx.enter_context(nc.sbuf_tensor(name, shape, dt))

        def sem(name):
            return ctx.enter_context(nc.semaphore(name))

        arena = sb("arena", [P, ITEMS], FP32)
        payload = arena[:, 0:4 * T].rearrange("p (t w) -> p t w", w=4)
        payload_i = payload.bitcast(I32)
        rows_i = arena[:, 4 * T:5 * T].bitcast(I32)
        cols_i = arena[:, 5 * T:6 * T].bitcast(I32)
        resident = arena[:, 0:4 * (K + RING)].bitcast(I32).rearrange("p (k w) -> p k w", w=4)
        below = arena[:, 4 * (K + RING):ITEMS].bitcast(BF16)[:, 0:UCOLS * TILES].rearrange(
            "p (j t) -> p j t", t=TILES)
        parts = arena[:, :].bitcast(BF16)
        items_12 = parts[:, 0:ITEMS]
        items_33 = parts[:, ITEMS:2 * ITEMS]
        rated = sb("rated", [P, MT, NB], FP32)
        flat = rated[:, :, :].rearrange("p m n -> p (m n)")
        vals_f = flat[:, 0:T]
        bits = flat[:, T:2 * T].bitcast(I32)
        new = sb("new", [P, TILES * F], FP32)
        total = sb("total", [P, TILES * F], FP32)
        new3 = new[:, :].rearrange("p (t f) -> p t f", f=F)
        items_3b = new[:, :].bitcast(BF16)[:, 0:ITEMS]
        flat_b = rated[:, :, :].rearrange("p m n -> p (m n)").bitcast(BF16)
        rest1 = flat[:, 0:1024].rearrange("p (n c) -> p n c", n=2)
        part2 = flat_b[:, 3072:4096].rearrange("p (n c) -> p n c", n=2)
        urest = flat[:, 2048:2048 + MT * P]
        hot_hl = total[:, 0:HSLOTS * HG * LOW].bitcast(BF16).rearrange(
            "p (s a g v c) -> p s a g v c", s=HSLOTS, a=2, v=LOW, c=PACK)
        high_i = total[:, HSLOTS * HG * LOW:HSLOTS * HG * LOW + T].bitcast(I32)
        low_i = total[:, HSLOTS * HG * LOW + T:HSLOTS * HG * LOW + 2 * T].bitcast(I32)
        high_b = flat_b[:, 2 * T:3 * T]
        low_b = flat_b[:, 3 * T:4 * T]
        mini = sb("mini", [P, TILES, MINI], FP32)
        fill_sb = sb("fill_sb", [P, K // RING, 4], I32)
        unit_off = sb("unit_off", [1, P * UCOLS], I32)
        gathered = sb("gathered", [P, RING, F], FP32)
        spread = sb("spread", [P, R_SLOTS, P], FP32)
        ring = sb("ring", [P, 2, LG, 4], I32)
        ring_f = ring[:, :, :, :].bitcast(FP32)
        pay = sb("pay", [P, 2, SG, 4], I32)
        pay_f = pay[:, :, :, :].bitcast(FP32)
        onehot = sb("onehot", [P, 2 * SG, TW], BF16)
        picked = sb("picked", [P, SG, TW], BF16)
        rank = sb("rank", [P, 2, SG], FP32)
        rank_i = sb("rank_i", [P, SG], I32)
        rank_lo = sb("rank_lo", [P, SG], I32)
        rank_hi = sb("rank_hi", [P, SG], I32)
        place = sb("place", [P, 2, SG], I32)
        iota_i = sb("iota_i", [P, TW], I32)
        lane_i = sb("lane_i", [P, 1], I32)
        lane_f = sb("lane_f", [P, 1], FP32)
        iota_t = sb("iota_t", [P, TW], BF16)
        iota_l = sb("iota_l", [P, P], FP32)
        ident = sb("ident", [P, P], FP32)
        ones = sb("ones", [P, P], BF16)
        earlier = sb("earlier", [P, P], BF16)
        not_earlier = sb("not_earlier", [P, P], BF16)
        zeros = sb("zeros", [P, TW], FP32)
        zeros_b = sb("zeros_b", [P, TW], BF16)
        ones_row = sb("ones_row", [1, P], FP32)
        filled = sb("filled", [P, TW], I32)
        units = sb("units", [P, TW], FP32)
        upto = sb("upto", [P, TW], FP32)
        base = sb("base", [P, 2, TW], FP32)
        unit_no = sb("unit_no", [P, UCOLS], I32)
        unit_tile = sb("unit_tile", [P, UCOLS], FP32)
        unit_word = sb("unit_word", [P, UCOLS], I32)
        who = sb("who", [P, MT], I32)
        who_f = sb("who_f", [P, 4, MT], FP32)
        who_i = sb("who_i", [P, 4, MT], I32)
        who_bias = sb("who_bias", [P, MT], FP32)
        who_emb = sb("who_emb", [P, MT, F], FP32)
        staging = onehot[:, :, :].rearrange("p c t -> p (c t)").bitcast(FP32)
        istage = staging[:, 0:1024].rearrange("p (n q o f) -> p n q o f", n=2, q=4, o=2)
        ustage = staging[:, 1024:2048].rearrange("p (m o f) -> p m o f", m=MT, o=2)
        spread_b = spread[:, :, :].rearrange("p r l -> p (r l)").bitcast(BF16)
        gathered_b = gathered[:, :, :].rearrange("p r f -> p (r f)").bitcast(BF16)
        u1 = spread_b[:, 0:MT * P]
        u2 = spread_b[:, MT * P:2 * MT * P]
        u3 = gathered_b[:, 0:MT * P]
        u12 = gathered_b[:, MT * P:2 * MT * P]
        u3b = sb("u3b", [P, MT * P], BF16)
        bias_f = sb("bias_f", [125, ITEMS // 125], FP32)
        bias_r = sb("bias_r", [125, ITEMS // 125], FP32)
        bias_p = sb("bias_p", [125, 3, ITEMS // 125], BF16)
        same_chunk = sb("same_chunk", [P, LOW, PACK], FP32)
        own_high = sb("own_high", [P, HIGH, LOW], FP32)
        group_i = sb("group_i", [P, 2], I32)
        group_f = sb("group_f", [P, 2], FP32)
        block_i = sb("block_i", [P, LOW, PACK], I32)
        blocks = sb("blocks", [P, LOW, PACK], FP32)
        diagonal = sb("diagonal", [P, LOW], FP32)
        by_tile = sb("by_tile", [P, HIGH, LOW], FP32)
        high_no = sb("high_no", [P, HIGH, LOW], I32)
        value_no = sb("value_no", [P, HG // PACK, LOW, PACK], BF16)
        ones_f = sb("ones_f", [P, P], FP32)

        psum = ctx.enter_context(nc.psum_tensor("psum", [P, 8, 512], FP32))
        pairs = psum[:, 2, 0:P]
        counts = psum[:, 0, 0:HIGH * LOW]
        running = psum[:, 1, 0:2 * TW]

        s_const = sem("s_const")
        s_blank = sem("s_blank")
        s_rows = sem("s_rows")
        s_cols = sem("s_cols")
        s_vals = sem("s_vals")
        s_emb = sem("s_emb")
        s_mini = sem("s_mini")
        s_x0 = sem("s_x0")
        s_dve = sem("s_dve")
        s_ready = sem("s_ready")
        s_fill = sem("s_fill")
        s_filled = sem("s_filled")
        s_hot = sem("s_hot")
        s_tiled = sem("s_tiled")
        s_counts = sem("s_counts")
        s_hotused = sem("s_hotused")
        s_base = sem("s_base")
        s_oh = sem("s_oh")
        s_ranked = sem("s_ranked")
        s_read = sem("s_read")
        s_copy = sem("s_copy")
        s_conv = sem("s_conv")
        s_place = sem("s_place")
        s_scat = [sem(f"s_scat{h}") for h in range(2)]
        s_pace = sem("s_pace")
        s_dvepace = sem("s_dvepace")
        s_uword = sem("s_uword")
        s_umap = sem("s_umap")
        s_uoff = sem("s_uoff")
        s_table = sem("s_table")
        s_tot = sem("s_tot")
        s_clean = sem("s_clean")
        s_head = sem("s_head")
        s_rest = sem("s_rest")
        s_pay = sem("s_pay")
        s_g = [sem(f"s_g{c}") for c in range(RING)]
        s_spread = sem("s_spread")
        s_chunk = sem("s_chunk")
        s_add = sem("s_add")
        s_who = sem("s_who")
        s_whoidx = sem("s_whoidx")
        s_whobias = sem("s_whobias")
        s_urows = sem("s_urows")
        s_uemb = sem("s_uemb")
        s_ut = sem("s_ut")
        s_stage = sem("s_stage")
        s_it = sem("s_it")
        s_bias = sem("s_bias")
        s_biasp = sem("s_biasp")
        s_biasd = sem("s_biasd")
        s_biast = sem("s_biast")
        s_part1 = sem("s_part1")
        s_rest1 = sem("s_rest1")
        s_part2 = sem("s_part2")
        s_part3 = sem("s_part3")
        s_placed = sem("s_placed")
        s_ustage = sem("s_ustage")
        s_u = sem("s_u")
        s_rate = sem("s_rate")
        s_sig = sem("s_sig")
        s_out = [sem(f"s_out{m}") for m in range(MT)]

        batches = [[(0, UTILES + 4 * n, 4)] for n in range(I_TILES // 4)] + [[(0, UTILES - 1, 1), (1, TILES - 2, 2)]]
        columns = [[(0, I_FIRST + 4 * P * n, 4 * P)] for n in range(I_TILES // 4)] + \
            [[(U_LANES, 0, I_FIRST), (P, ITEMS - I_LAST - P, P + I_LAST)]]

        def piece_of(n):
            return max(k + 1 for k, (a, b) in enumerate(PIECES) for _, t, m in batches[n] if t < b and a < t + m)

        def width(n):
            return sum(k for _, _, k in batches[n]) * P

        block = ctx.enter_context(nc.Block())

        @block.sync
        def _(sp):
            sp.wait_ge(s_blank, 1)
            sp.dma_start(rows_i[0:P - 1, :], rows[0:(P - 1) * T].rearrange("(p t) -> p t", t=T)).then_inc(s_rows, 16)
            sp.dma_start(rows_i[P - 1:P, 0:LAST_E], rows[(P - 1) * T:NNZ].rearrange("(p t) -> p t", p=1)).then_inc(s_rows, 16)
            sp.wait_ge(s_blank, 2)
            sp.dma_start(cols_i[0:P - 1, :], cols[0:(P - 1) * T].rearrange("(p t) -> p t", t=T)).then_inc(s_cols, 16)
            sp.dma_start(cols_i[P - 1:P, 0:LAST_E], cols[(P - 1) * T:NNZ].rearrange("(p t) -> p t", p=1)).then_inc(s_cols, 16)
            sp.wait_ge(s_fill, 2)
            for n in range(RING):
                w = 4 * (K // RING)
                sp.dma_start(slots_v[:, n * w:(n + 1) * w], fill_sb[:, :, :].rearrange("p k w -> p (k w)")).then_inc(s_filled, 16)
            sp.wait_ge(s_blank, 4)
            for dst, ue, ie, s in ((new3, emb_u, emb_i, s_emb), (mini[:, :, :], mm_u, mm_i, s_mini)):
                sp.dma_start(dst[:, 0:UTILES - 1, :], ue[0:(UTILES - 1) * P, :].rearrange("(t p) f -> p t f", p=P)).then_inc(s, 16)
                sp.dma_start(dst[0:U_LANES, UTILES - 1, :], ue[(UTILES - 1) * P:USERS, :]).then_inc(s, 16)
                sp.dma_start(dst[U_LANES:P, UTILES - 1, :], ie[0:I_FIRST, :]).then_inc(s, 16)
                sp.dma_start(dst[:, UTILES:UTILES + I_TILES, :], ie[I_FIRST:I_FIRST + I_TILES * P, :].rearrange("(t p) f -> p t f", p=P)).then_inc(s, 16)
                sp.dma_start(dst[0:I_LAST, TILES - 1, :], ie[I_FIRST + I_TILES * P:ITEMS, :]).then_inc(s, 16)
            sp.wait_ge(s_x0, X0_ITERS)
            sp.dma_start(table_v, new[:, :]).then_inc(s_table, 16)
            sp.wait_ge(s_uword, 1)
            sp.dma_start(unit_map[:, :], unit_word[:, :]).then_inc(s_umap, 16)
            sp.wait_ge(s_umap, 16)
            sp.dma_start(unit_off[0:1, :], unit_map.rearrange("(o p) j -> o (p j)", o=1)).then_inc(s_uoff, 16)
            sp.wait_ge(s_biasp, 1)
            for k in range(3):
                sp.dma_start(bias_parts[k:k + 1, :].rearrange("o (p n) -> (o p) n", p=125), bias_p[:, k, :]).then_inc(s_biasd, 16)
            for h in range(2):
                sp.wait_ge(s_scat[h], 16 * SG * SORT_ITERS)
            res = arena[:, 0:4 * (K + RING)].bitcast(I32)
            sp.dma_start(res[:, 0:4 * RING], slots_v[:, 0:4 * RING]).then_inc(s_head, 16)
            sp.dma_start(res[:, 4 * RING:4 * K], slots_v[:, 4 * RING:4 * K]).then_inc(s_rest, 16)
            sp.dma_start(res[:, 4 * K:4 * (K + RING)], slots_v[:, 0:4 * RING]).then_inc(s_rest, 16)
            with sp.Fori(1, LAYERS) as layer:
                sp.wait_ge(s_add, layer * (K * UNITS) + UNITS * PS_SLOTS)
                sp.dma_start(table_v, new[:, :]).then_inc(s_table, 16)
            sp.wait_ge(s_tot, TOT_DONE)
            sp.dma_start(user_rows.rearrange("(p t) f -> p (t f)", p=P), total[:, 0:UTILES * F]).then_inc(s_urows, 16)
            sp.wait_ge(s_biasd, 48)
            sp.dma_start(items_3b[F:F + 3, :], bias_parts[:, :]).then_inc(s_biast, 16)
            with sp.Fori(0, ITEMS // NB) as j:
                for m in range(MT):
                    sp.wait_ge(s_sig, j * MT + (MT + m + 1))
                    sp.dma_start(out_v[:, m, bass.ds(j * NB, NB)], rated[:, m, :]).then_inc(s_out[m], 16)
            for m in range(MT):
                sp.wait_ge(s_out[m], 16 * (ITEMS // NB))

        @block.scalar
        def _(act):
            act.wait_ge(s_blank, 3)
            act.dma_start(vals_f[0:P - 1, :], vals[0:(P - 1) * T].rearrange("(p t) -> p t", t=T)).then_inc(s_vals, 16)
            act.dma_start(vals_f[P - 1:P, 0:LAST_E], vals[(P - 1) * T:NNZ].rearrange("(p t) -> p t", p=1)).then_inc(s_vals, 16)
            act.dma_start(bias_f[:, :], bias_i.rearrange("(p n) -> p n", p=125)).then_inc(s_bias, 16)
            act.dma_start(who[:, :], users.rearrange("(p m) -> p m", m=MT)).then_inc(s_who, 16)

            def stage(n):
                act.wait_ge(s_tot, TOT_DONE - len(PIECES) + piece_of(n))
                if n >= 2:
                    act.wait_ge(s_it, n - 1)
                for q, t, k in batches[n]:
                    last = nc.scalar.activation(
                        istage[:, n % 2, q:q + k, :, :],
                        total[:, t * F:(t + k) * F].rearrange("p (t o f) -> p t o f", t=k, o=1).broadcast_to([P, k, 2, F]),
                        ACT.Copy, scale=1.0 / (LAYERS + 1))
                last.then_inc(s_stage, 1)

            def second(n):
                act.wait_ge(s_rest1, n + 1)
                w = width(n)
                if n >= 2:
                    act.wait_ge(s_placed, n - 1)
                nc.scalar.activation(part2[:, n % 2, 0:w], rest1[:, n % 2, 0:w], ACT.Copy).then_inc(s_part2, 1)

            stage(0)
            stage(1)
            for n in range(len(batches)):
                act.wait_ge(s_it, n + 1)
                for c, a, w in columns[n]:
                    last = nc.scalar.activation(items_12[:, a:a + w], psum[:, n % 2, c:c + w], ACT.Copy)
                last.then_inc(s_part1, 1)
                if n >= 1:
                    second(n - 1)
                if n + 2 < len(batches):
                    stage(n + 2)
            second(len(batches) - 1)
            act.wait_ge(s_uemb, 16 * MT)
            nc.scalar.activation(ustage, who_emb[:, :, :].rearrange("p m (o f) -> p m o f", o=1).broadcast_to([P, MT, 2, F]),
                                 ACT.Copy, scale=1.0 / (LAYERS + 1)).then_inc(s_ustage, 1)
            act.wait_ge(s_whobias, 16 * MT)
            act.sem_inc(s_sig, MT)

            def rate(j, first):
                for m in range(MT):
                    act.wait_ge(s_rate, j * MT + (m + 1))
                    if not first:
                        act.wait_ge(s_out[m], j * 16)
                    nc.scalar.activation(rated[:, m, :], psum[:, m, 0:NB], ACT.Sigmoid,
                                         bias=who_bias[:, m:m + 1]).then_inc(s_sig, 1)

            rate(0, True)
            with act.Fori(1, ITEMS // NB) as j:
                rate(j, False)

        @block.gpsimd
        def _(pool):
            pool.iota(iota_i[:, :], pattern=[[1, TW]], base=0, channel_multiplier=0).then_inc(s_const, 1)
            pool.iota(lane_i[:, :], pattern=[[1, 1]], base=0, channel_multiplier=1).then_inc(s_const, 1)
            pool.iota(block_i[:, :, :], pattern=[[0, LOW], [1, PACK]], base=0, channel_multiplier=0).then_inc(s_const, 1)
            pool.iota(high_no[:, :, :], pattern=[[1, HIGH], [0, LOW]], base=0, channel_multiplier=0).then_inc(s_const, 1)
            pool.iota(unit_no[:, :], pattern=[[1, UCOLS]], base=0, channel_multiplier=UCOLS).then_inc(s_const, 1)
            for q in range(HSLOTS):
                pool.memset(hot_hl[:, q, 0, :, HIGH:LOW, :], 0.0).then_inc(s_const, 1)
            pool.memset(fill_sb[:, :, 1:4], 0).then_inc(s_fill, 1)
            pool.memset(fill_sb[:, :, 0:1], ZERO_ROW).then_inc(s_fill, 1)
            pool.wait_ge(s_filled, 16 * RING)
            with pool.Fori(0, SORT_ITERS) as i:
                for h in range(2):
                    pool.wait_ge(s_place, i * 2 + (h + 1))
                    pool.sem_inc(s_pace, 1)
                    for c in range(SG):
                        pool.indirect_dma_start(
                            out=slots[:, :], out_offset=bass.IndirectOffsetOnAxis(ap=place[:, h, c:c + 1], axis=0),
                            in_=pay[:, h, c, :], in_offset=None).then_inc(s_scat[h], 16)
            with pool.Fori(0, LAYERS) as layer:
                pool.wait_ge(s_table, layer * 16 + 16)
                pool.sem_inc(s_pace, 1)
                with pool.Fori(0, LAYER_ITERS) as i:
                    for h in range(2):
                        pool.wait_ge(s_pay, (layer * LAYER_ITERS + i) * 2 + (h + 1))
                        pool.sem_inc(s_pace, 1)
                        for c in range(LG):
                            pool.indirect_dma_start(
                                out=gathered[:, h * LG + c, :], out_offset=None, in_=table[:, :],
                                in_offset=bass.IndirectOffsetOnAxis(ap=ring[:, h, c, 0:1], axis=0)).then_inc(s_g[h * LG + c], 16)
            pool.wait_ge(s_whoidx, 1)
            for m in range(MT):
                pool.indirect_dma_start(
                    out=who_bias[:, m:m + 1], out_offset=None, in_=bias_u[:, :],
                    in_offset=bass.IndirectOffsetOnAxis(ap=who_i[:, 0, m:m + 1], axis=0)).then_inc(s_whobias, 16)
            pool.wait_ge(s_urows, 16)
            for m in range(MT):
                pool.indirect_dma_start(
                    out=who_emb[:, m, :], out_offset=None, in_=user_rows[:, :],
                    in_offset=bass.IndirectOffsetOnAxis(ap=who_i[:, 3, m:m + 1], axis=0)).then_inc(s_uemb, 16)

        @block.vector
        def _(dve):
            chain = [0]

            def link(ins):
                chain[0] += 1
                ins.then_inc(s_dve, 1)
                dve.wait_ge(s_dve, chain[0])

            nc.vector.memset(rows_i[96:P, LAST_E:T], ZERO_ROW).then_inc(s_blank, 1)
            nc.vector.memset(cols_i[96:P, LAST_E:T], ZERO_ROW).then_inc(s_blank, 1)
            nc.vector.memset(vals_f[96:P, LAST_E:T], 0.0).then_inc(s_blank, 1)
            nc.vector.memset(new3[:, TILES - 1, :], 0.0)
            nc.vector.memset(mini[:, TILES - 1, :], 0.0)
            link(nc.vector.memset(ones_row[:, :], 1.0))
            dve.sem_inc(s_blank, 1)
            nc.vector.memset(ones[:, :], 1.0)
            nc.vector.memset(zeros[:, :], 0.0)
            nc.vector.memset(zeros_b[:, :], 0.0)
            nc.vector.memset(u3b[F:F + 3, :], 1.0)
            dve.wait_ge(s_const, 5 + HSLOTS)
            nc.vector.tensor_copy(lane_f[:, :], lane_i[:, :])
            nc.vector.tensor_copy(iota_t[:, :], iota_i[:, :])
            link(nc.vector.tensor_copy(iota_l[:, :], iota_i[:, 0:P]))
            for g in range(HG // PACK):
                nc.vector.tensor_copy(value_no[:, g, :, :], iota_l[:, 0:LOW].rearrange("p (v o) -> p v o", o=1).broadcast_to([P, LOW, PACK]))
            nc.vector.tensor_scalar(ident[:, :], iota_l[:, :], lane_f[:, 0:1], None, ALU.is_equal)
            nc.vector.tensor_scalar(earlier[:, :], iota_l[:, :], lane_f[:, 0:1], None, ALU.is_gt)
            nc.vector.tensor_scalar(not_earlier[:, :], iota_l[:, :], lane_f[:, 0:1], None, ALU.is_le).then_inc(s_ready, 1)

            nc.vector.tensor_scalar(group_i[:, 0:1], lane_i[:, :], PACK - 1, None, ALU.bitwise_and)
            nc.vector.tensor_scalar(group_i[:, 1:2], lane_i[:, :], PACK.bit_length() - 1, None, ALU.logical_shift_right)
            link(nc.vector.memset(ones_f[:, :], 1.0))
            link(nc.vector.tensor_copy(group_f[:, :], group_i[:, :]))
            nc.vector.tensor_scalar(same_chunk[:, :, :], block_i[:, :, :], group_f[:, 0:1], None, ALU.is_equal)
            nc.vector.tensor_scalar(own_high[:, :, :], high_no[:, :, :], group_f[:, 1:2], None, ALU.is_equal)

            dve.wait_ge(s_rows, 32)
            nc.vector.tensor_scalar(high_i, rows_i, 7 + LOW.bit_length() - 1, None, ALU.logical_shift_right)
            link(nc.vector.tensor_scalar(low_i, rows_i, 7, LOW - 1, ALU.logical_shift_right, ALU.bitwise_and))
            nc.vector.tensor_copy(high_b, high_i)
            link(nc.vector.tensor_copy(low_b, low_i))

            def hot_group(i, q, first):
                if not first:
                    dve.wait_ge(s_hotused, i * HSLOTS + (q + 1 - HSLOTS))
                for a, (of, most) in enumerate(((high_b, HIGH), (low_b, LOW))):
                    of = of[:, bass.ds(i * (HG * HSLOTS) + q * HG, HG)].rearrange("p (g o c) -> p g o c", o=1, c=PACK)
                    last = nc.vector.tensor_tensor(hot_hl[:, q, a, :, 0:most, :], of.broadcast_to([P, HG // PACK, most, PACK]),
                                                   value_no[:, :, 0:most, :], ALU.is_equal)
                last.then_inc(s_hot, 1)

            for q in range(HSLOTS):
                hot_group(0, q, True)
            with dve.Fori(1, HIST_ITERS) as i:
                for q in range(HSLOTS):
                    hot_group(i, q, False)

            dve.wait_ge(s_vals, 32)
            nc.vector.tensor_copy(payload[:, :, 1], vals_f)
            dve.wait_ge(s_hot, HIST_ITERS * HSLOTS)
            link(nc.vector.tensor_scalar(bits, rows_i, 7, None, ALU.logical_shift_right))
            link(nc.vector.tensor_copy(payload[:, :, 3], bits))
            link(nc.vector.tensor_scalar(bits, rows_i, P - 1, None, ALU.bitwise_and))
            link(nc.vector.tensor_copy(payload[:, :, 2], bits))
            dve.wait_ge(s_cols, 32)
            nc.vector.tensor_scalar(bits, cols_i, 7, None, ALU.logical_shift_right)
            link(nc.vector.tensor_scalar(rows_i, cols_i, P - 1, None, ALU.bitwise_and))
            link(nc.vector.scalar_tensor_tensor(payload_i[:, :, 0], rows_i, float(TILES), bits, ALU.mult, ALU.add))

            dve.wait_ge(s_hotused, HIST_ITERS * HSLOTS)
            link(nc.vector.tensor_tensor(blocks[:, :, :], pairs.rearrange("p (v c) -> p v c", c=PACK), same_chunk[:, :, :], ALU.mult))
            link(nc.vector.tensor_reduce(diagonal[:, :], blocks[:, :, :], AX.X, ALU.add))
            nc.vector.tensor_tensor(by_tile[:, :, :], own_high[:, :, :],
                                    diagonal[:, :].rearrange("p (o v) -> p o v", o=1).broadcast_to([P, HIGH, LOW]),
                                    ALU.mult).then_inc(s_tiled, 1)
            dve.wait_ge(s_counts, 1)
            link(nc.vector.tensor_scalar(filled[:, :], counts[:, 0:TW], float(UNIT - 1), None, ALU.add))
            link(nc.vector.tensor_scalar(filled[:, :], filled[:, :], UNIT.bit_length() - 1, None, ALU.logical_shift_right))
            link(nc.vector.tensor_copy(units[:, :], filled[:, :]))
            link(nc.vector.tensor_tensor_scan(upto[:, :], units[:, :], zeros[:, :], 0.0, ALU.add, ALU.add))
            link(nc.vector.tensor_tensor(base[:, 0, :], upto[:, :], units[:, :], ALU.subtract))
            nc.vector.tensor_scalar(base[:, 1, :], base[:, 0, :], float(UNIT), None, ALU.mult)
            nc.vector.tensor_scalar(base[:, 0, :], base[:, 0, :], float(UNIT), None, ALU.mult).then_inc(s_base, 1)

            def hot(h, c):
                nc.vector.tensor_scalar(onehot[:, c, :], iota_t[:, :], pay_f[:, h, c, 3:4], None,
                                        ALU.is_equal)
                nc.vector.tensor_scalar(onehot[:, c + 1, :], iota_t[:, :], pay_f[:, h, c + 1, 3:4], None,
                                        ALU.is_equal).then_inc(s_oh, 1)

            def rank_group(i, h, first):
                if not first:
                    dve.wait_ge(s_scat[h], i * (16 * SG))
                nc.vector.tensor_copy(pay[:, h, :, :], payload_i[:, bass.ds(i * (2 * SG) + h * SG, SG), :]).then_inc(s_copy, 1)
                dve.wait_ge(s_copy, i * 2 + (h + 1))
                hot(h, 0)
                for c in range(0, SG, 2):
                    if c + 2 < SG:
                        hot(h, c + 2)
                    dve.wait_ge(s_ranked, i * SG + (h * SG + c) // 2 + 1)
                    for e in range(2):
                        last = nc.vector.tensor_tensor_reduce(
                            out=picked[:, c + e, :], in0=running[:, e * TW:(e + 1) * TW], in1=onehot[:, c + e, :], scale=1.0,
                            scalar=0.0, op0=ALU.mult, op1=ALU.add, accum_out=rank[:, h, c + e:c + e + 1])
                    last.then_inc(s_read, 1)
                dve.wait_ge(s_read, i * SG + (h + 1) * SG // 2)
                nc.vector.tensor_copy(rank_i[:, :], rank[:, h, :]).then_inc(s_conv, 1)
                dve.wait_ge(s_conv, (i * 2 + h) * 2 + 1)
                nc.vector.tensor_scalar(rank_lo[:, :], rank_i[:, :], P - 1, None, ALU.bitwise_and)
                nc.vector.tensor_scalar(rank_hi[:, :], rank_i[:, :], 7, None, ALU.logical_shift_right).then_inc(s_conv, 1)
                dve.wait_ge(s_conv, (i * 2 + h) * 2 + 2)
                nc.vector.scalar_tensor_tensor(place[:, h, :], rank_lo[:, :], float(K), rank_hi[:, :],
                                               ALU.mult, ALU.add).then_inc(s_place, 1)

            for h in range(2):
                rank_group(0, h, True)
            dve.wait_ge(s_emb, 16 * 5)
            dve.wait_ge(s_mini, 16 * 5)
            new4 = new[:, :].rearrange("p (t r) -> p t r", r=F // MINI)
            small = mini[:, :, :].rearrange("p t (f o) -> p (t f) o", o=1)
            w = X0_TILES * MINI
            with dve.Fori(1, X0_ITERS + 1) as i:
                for h in range(2):
                    rank_group(i, h, False)
                    if h == 0:
                        part = bass.ds(i * w - w, w)
                        nc.vector.tensor_tensor(new4[:, part, :], new4[:, part, :],
                                                small[:, part, :].broadcast_to([P, w, F // MINI]), ALU.add).then_inc(s_x0, 1)
            with dve.Fori(X0_ITERS + 1, SORT_ITERS) as i:
                for h in range(2):
                    rank_group(i, h, False)

            n_b = unit_no[:, :].rearrange("p (j o) -> p j o", o=1).broadcast_to([P, UCOLS, TILES])
            u_b = upto[:, 0:TILES].rearrange("p (o t) -> p o t", o=1).broadcast_to([P, UCOLS, TILES])
            link(nc.vector.tensor_tensor(below, u_b, n_b, ALU.is_le))
            link(nc.vector.tensor_reduce(unit_tile[:, :], below, AX.X, ALU.add))
            nc.vector.tensor_scalar(unit_word[:, :], unit_tile[:, :], float(TILES - 1), float(F),
                                    ALU.min, ALU.mult).then_inc(s_uword, 1)

            dve.wait_ge(s_who, 16)
            link(nc.vector.tensor_copy(who_f[:, 0, :], who[:, :]))
            link(nc.vector.tensor_scalar(who_f[:, 1, :], who_f[:, 0, :], 0.0, float(USERS), ALU.is_lt, ALU.mult))
            link(nc.vector.tensor_tensor(who_f[:, 2, :], who_f[:, 0, :], who_f[:, 1, :], ALU.add))
            link(nc.vector.tensor_scalar(who_i[:, 0, :], who_f[:, 2, :], 0.0, float(USERS - 1), ALU.max, ALU.min))
            nc.vector.tensor_scalar(who_i[:, 1, :], who_i[:, 0, :], P - 1, None, ALU.bitwise_and)
            link(nc.vector.tensor_scalar(who_i[:, 2, :], who_i[:, 0, :], 7, None, ALU.logical_shift_right))
            nc.vector.scalar_tensor_tensor(who_i[:, 3, :], who_i[:, 1, :], float(UTILES), who_i[:, 2, :],
                                           ALU.mult, ALU.add).then_inc(s_whoidx, 1)

            dve.wait_ge(s_bias, 16)
            link(nc.vector.tensor_copy(bias_p[:, 0, :], bias_f[:, :]))
            link(nc.vector.tensor_tensor(bias_r[:, :], bias_f[:, :], bias_p[:, 0, :], ALU.subtract))
            link(nc.vector.tensor_copy(bias_p[:, 1, :], bias_r[:, :]))
            nc.vector.tensor_tensor(bias_p[:, 2, :], bias_r[:, :], bias_p[:, 1, :], ALU.subtract).then_inc(s_biasp, 1)

            dve.wait_ge(s_x0, X0_ITERS)
            nc.vector.tensor_copy(total[:, :], new[:, :]).then_inc(s_tot, 1)
            dve.sem_inc(s_add, UNITS * PS_SLOTS)
            dve.wait_ge(s_head, 16)
            for h in range(2):
                nc.vector.tensor_copy(ring[:, h, :, :], resident[:, h * LG:(h + 1) * LG, :]).then_inc(s_pay, 1)

            def values(n):
                h, c = n // LG % 2, n % LG
                nc.vector.tensor_scalar(spread[:, n % R_SLOTS, :], iota_l[:, :], ring_f[:, h, c, 2:3],
                                        ring_f[:, h, c, 1:2], ALU.is_equal, ALU.mult).then_inc(s_spread, 1)

            dve.wait_ge(s_pay, 1)
            for n in range(AHEAD):
                values(n)
            dve.wait_ge(s_rest, 32)
            dve.wait_ge(s_uoff, 16)

            with dve.Fori(0, LAYERS) as layer:
                dve.wait_ge(s_table, layer * 16 + 16)
                dve.wait_ge(s_tot, layer * len(PIECES) + 1)
                nc.vector.memset(new[:, :], 0.0).then_inc(s_clean, 1)
                dve.wait_ge(s_clean, layer + 1)
                dve.sem_inc(s_dvepace, 1)
                with dve.Fori(0, LAYER_ITERS) as i:
                    done = (layer * LAYER_ITERS + i) * RING

                    for h in range(2):
                        dve.wait_ge(s_pay, (layer * LAYER_ITERS + i) * 2 + (h + 2))
                        _, at = nc.values_load_multi_w_load_instructions(
                            unit_off[0:1, bass.ds(i * (RING * UNITS) + h * LG * UNITS, LG * UNITS)],
                            engines=(mybir.EngineType.DVE,), min_val=0, max_val=(TILES - 1) * F,
                            skip_runtime_bounds_check_because="the chip clamps each to (TILES - 1) * F above")
                        for c in range(0, LG, 2):
                            n = h * LG + c
                            dve.wait_ge(s_chunk, done + (n + 2))
                            for k in range(2 * UNITS):
                                dve.wait_ge(s_add, done * UNITS + (UNITS * (PS_SLOTS + n) + k))
                                tile = new[:, bass.ds(at[c * UNITS + k], F)]
                                nc.vector.tensor_tensor(tile, tile, psum[:, (n % PS_SLOTS) * UNITS + k, 0:F],
                                                        ALU.add).then_inc(s_add, 1)
                                if k < 2:
                                    values(n + AHEAD + k)
                        nc.vector.tensor_copy(ring[:, h, :, :], resident[:, bass.ds(i * RING + (RING + h * LG), LG), :]).then_inc(s_pay, 1)
                dve.wait_ge(s_add, (layer + 1) * (K * UNITS) + UNITS * PS_SLOTS)
                for a, b in PIECES:
                    nc.vector.tensor_tensor(total[:, a * F:b * F], total[:, a * F:b * F], new[:, a * F:b * F],
                                            ALU.add).then_inc(s_tot, 1)

            dve.wait_ge(s_tot, TOT_DONE)
            def third(n):
                dve.wait_ge(s_part2, n + 1)
                for c, a, w in columns[n]:
                    nc.vector.tensor_copy(items_12[F:P, a:a + w], part2[F:P, n % 2, c:c + w])
                    last = nc.vector.tensor_tensor(items_33[:, a:a + w], rest1[:, n % 2, c:c + w],
                                                   part2[:, n % 2, c:c + w], ALU.subtract)
                last.then_inc(s_part3, 1)
                dve.wait_ge(s_part3, n + 1)
                for c, a, w in columns[n]:
                    last = nc.vector.tensor_copy(items_3b[0:F, a:a + w], items_33[0:F, a:a + w])
                last.then_inc(s_placed, 1)

            for n in range(len(batches)):
                dve.wait_ge(s_part1, n + 1)
                for c, a, w in columns[n]:
                    last = nc.vector.tensor_tensor(rest1[:, n % 2, c:c + w], psum[:, n % 2, c:c + w],
                                                   items_12[:, a:a + w], ALU.subtract)
                last.then_inc(s_rest1, 1)
                if n >= 1:
                    third(n - 1)
            third(len(batches) - 1)
            dve.wait_ge(s_ut, 1)
            users_p = psum[:, 2:4, :].rearrange("p a c -> p (a c)")
            link(nc.vector.tensor_copy(u1, users_p))
            link(nc.vector.tensor_tensor(urest, users_p, u1, ALU.subtract))
            link(nc.vector.tensor_copy(u2, urest))
            nc.vector.tensor_copy(u12[0:F, :], u1[0:F, :])
            nc.vector.tensor_copy(u12[F:P, :], u2[F:P, :])
            link(nc.vector.tensor_tensor(u3, urest, u2, ALU.subtract))
            nc.vector.tensor_copy(u3b[0:F, :], u3[0:F, :]).then_inc(s_u, 1)

        @block.tensor
        def _(pe):
            pe.wait_ge(s_ready, 1)
            pe.matmul(pairs, ones[:, :], zeros_b[:, 0:P], start=True, stop=True, skip_group_check=True)
            with pe.Fori(0, HIST_ITERS) as i:
                for q in range(HSLOTS):
                    pe.wait_ge(s_hot, i * HSLOTS + (q + 1))
                    for g in range(HG // PACK):
                        high, low = (hot_hl[:, q, a, g, :, :].rearrange("p v c -> p (v c)") for a in range(2))
                        last = pe.matmul(pairs, high, low, start=False, stop=True, skip_group_check=True)
                    last.then_inc(s_hotused, 1)
            pe.wait_ge(s_tiled, 1)
            pe.matmul(counts, ones_f[:, :], by_tile[:, :, :].rearrange("p h l -> p (h l)"), start=True, stop=True).then_inc(s_counts, 1)
            pe.wait_ge(s_base, 1)
            pe.matmul(running, ones_row[:, :], base[0:1, :, :].rearrange("p a t -> p (a t)"), start=True, stop=True, skip_group_check=True)
            with pe.Fori(0, SORT_ITERS) as i:
                for h in range(2):
                    for c in range(0, SG, 2):
                        n = (h * SG + c) // 2 + 1
                        pair = onehot[:, c:c + 2, :].rearrange("p a t -> p (a t)")
                        pe.wait_ge(s_oh, i * SG + n)
                        pe.matmul(running, earlier[:, :], pair, start=False, stop=True, skip_group_check=True)
                        pe.matmul(running[:, TW:2 * TW], ones[:, :], onehot[:, c, :], start=False, stop=True, skip_group_check=True).then_inc(s_ranked, 1)
                        pe.wait_ge(s_read, i * SG + n)
                        pe.matmul(running, not_earlier[:, :], pair, start=False, stop=True, skip_group_check=True)
                        pe.matmul(running[:, 0:TW], ones[:, :], onehot[:, c + 1, :], start=False, stop=True, skip_group_check=True)
            with pe.Fori(0, LAYERS) as layer:
                with pe.Fori(0, LAYER_ITERS) as i:
                    done = (layer * LAYER_ITERS + i) * RING
                    for n in range(RING):
                        pe.wait_ge(s_spread, done + (n + 1))
                        pe.wait_ge(s_g[n], (layer * LAYER_ITERS + i) * 16 + 16)
                        pe.wait_ge(s_add, done * UNITS + UNITS * (n + 1))
                        for u in range(UNITS):
                            a, b = u * UNIT, (u + 1) * UNIT
                            last = pe.matmul(psum[:, (n % PS_SLOTS) * UNITS + u, 0:F], spread[a:b, n % R_SLOTS, :],
                                             gathered[a:b, n, :], start=True, stop=True)
                        last.then_inc(s_chunk, 1)
            for n in range(len(batches)):
                pe.wait_ge(s_stage, n + 1)
                if n >= 2:
                    pe.wait_ge(s_rest1, n - 1)
                for q in range(width(n) // P):
                    last = pe.transpose(psum[:, n % 2, q * P:(q + 1) * P],
                                        istage[:, n % 2, q, :, :].rearrange("p o f -> p (o f)"), ident[:, :])
                last.then_inc(s_it, 1)
            pe.wait_ge(s_ustage, 1)
            for m in range(MT):
                last = pe.transpose(psum[:, 2 + m // 4, m % 4 * P:(m % 4 + 1) * P],
                                    ustage[:, m, :, :].rearrange("p o f -> p (o f)"), ident[:, :])
            last.then_inc(s_ut, 1)
            pe.wait_ge(s_placed, len(batches))
            pe.wait_ge(s_u, 1)
            pe.wait_ge(s_biast, 16)
            with pe.Fori(0, ITEMS // NB) as j:
                cols_j = bass.ds(j * NB, NB)
                for m in range(MT):
                    pe.wait_ge(s_sig, j * MT + (m + 1))
                    of, rows_m = psum[:, m, 0:NB], slice(m * P, (m + 1) * P)
                    pe.matmul(of, u1[:, rows_m], items_12[:, cols_j], start=True, stop=False)
                    pe.matmul(of, u2[:, rows_m], items_12[:, cols_j], start=False, stop=False)
                    pe.matmul(of, u3[:, rows_m], items_12[:, cols_j], start=False, stop=False)
                    pe.matmul(of, u12[:, rows_m], items_33[:, cols_j], start=False, stop=False)
                    pe.matmul(of, u3b[0:F + 3, rows_m], items_3b[0:F + 3, cols_j], start=False, stop=True).then_inc(s_rate, 1)


_INS = ["r_users", "L0_rec_emb_user", "L0_rec_emb_item", "L0_rec_bias_user", "L0_rec_bias_item",
        "L0_rec_mm_emb_user", "L0_rec_mm_emb_item", "L0_rec_graph_vals", "L0_rec_graph_rows",
        "L0_rec_graph_cols"]


def kernel(**inputs):
    import numpy as _np
    import concourse.bacc as _bacc
    from concourse import mybir as _mybir
    from concourse.bass_utils import run_bass_kernel_spmd as _run

    nc = _bacc.Bacc("TRN2", target_bir_lowering=False, num_devices=1)
    arrays, args = {}, []
    for name in _INS:
        a = _np.ascontiguousarray(inputs[name])
        if name == "L0_rec_bias_item":
            a = a.reshape(-1)
        arrays[name] = a
        args.append(nc.dram_tensor(name, a.shape, _mybir.dt.from_np(a.dtype), kind="ExternalInput").ap())
    args.append(nc.dram_tensor("out", (BATCH, ITEMS), _mybir.dt.float32, kind="ExternalOutput").ap())
    build(nc, *args)
    r = _run(nc, [arrays], core_ids=[0])
    return r.results[0]["out"]
```
